# Optimizing a Trainium2 kernel written in Bass

```python
import numpy as np
import jax
import jax.numpy as jnp

def _softmax(x, axis=-1):
    return jax.nn.softmax(x, axis=axis)

def _gelu(x):
    return jax.nn.gelu(x, approximate=True)

def _silu(x):
    return jax.nn.silu(x)

def _sigmoid(x):
    return jax.nn.sigmoid(x)

def _layernorm(x, axis=-1, eps=1e-05):
    m = jnp.mean(x, axis=axis, keepdims=True)
    v = jnp.var(x, axis=axis, keepdims=True)
    return (x - m) / jnp.sqrt(v + eps)

def _scatter_add(tgt, idx, src, axis=0):
    return tgt.at[idx].add(src)

def _segment_sum(src, seg, n):
    return jax.ops.segment_sum(src, seg, n)
kernel_name = 'mk_adaln_d1_jaxref_r4_7a496e'

def setup_inputs(seed: int=0):
    np.random.seed(seed)
    _w = jnp.asarray

    def _L0_attn_setup():
        import jax, jax.numpy as jnp
        import numpy as np
        BLOCK_H = 32
        BLOCK_W = 32
        N_FEAT = 1024
        K_FEAT = 1024
        key = jax.random.key(seed)
        k1, k2, k3 = jax.random.split(key, 3)
        data = jax.random.normal(k1, (4, 256, K_FEAT), dtype=jnp.float32)
        weight = jax.random.normal(k2, (N_FEAT, K_FEAT), dtype=jnp.float32) * 0.02
        nb, kb = (N_FEAT // BLOCK_H, K_FEAT // BLOCK_W)
        block_pattern = jax.random.randint(k3, (nb, kb), 0, 2, dtype=jnp.int32)
        mask = jnp.repeat(jnp.repeat(block_pattern, BLOCK_H, axis=0), BLOCK_W, axis=1)
        return {'data': data, 'weight': weight, 'mask': mask}
    _L0_attn_in = _L0_attn_setup()

    def _L0_ffn_setup():
        import jax, jax.numpy as jnp
        import numpy as np
        BLOCK = 64
        NF4_TABLE = jnp.array([-1.0, -0.6961928009986877, -0.5250730514526367, -0.39491748809814453, -0.28444138169288635, -0.18477343022823334, -0.09105003625154495, 0.0, 0.07958029955625534, 0.16093020141124725, 0.24611230194568634, 0.33791524171829224, 0.44070982933044434, 0.5626170039176941, 0.7229568362236023, 1.0], dtype=jnp.float32)
        D_MODEL, HIDDEN = (1024, 2752)
        BATCH, SEQ = (2, 512)

        def dequant_nf4(q, scale):
            O, I = q.shape
            vals = NF4_TABLE[q]
            vals = vals.reshape(O, I // BLOCK, BLOCK) * scale[:, :, None]
            return vals.reshape(O, I)
        key = jax.random.key(seed)
        ks = jax.random.split(key, 7)
        x = jax.random.normal(ks[0], (BATCH, SEQ, D_MODEL), dtype=jnp.float32)
        w1_q = jax.random.randint(ks[1], (HIDDEN, D_MODEL), 0, 16, dtype=jnp.int32)
        w2_q = jax.random.randint(ks[2], (HIDDEN, D_MODEL), 0, 16, dtype=jnp.int32)
        w3_q = jax.random.randint(ks[3], (D_MODEL, HIDDEN), 0, 16, dtype=jnp.int32)
        w1_scale = jax.random.uniform(ks[4], (HIDDEN, D_MODEL // BLOCK), dtype=jnp.float32) * 0.04
        w2_scale = jax.random.uniform(ks[5], (HIDDEN, D_MODEL // BLOCK), dtype=jnp.float32) * 0.04
        w3_scale = jax.random.uniform(ks[6], (D_MODEL, HIDDEN // BLOCK), dtype=jnp.float32) * 0.04
        return {'x': x, 'w1_q': w1_q, 'w1_scale': w1_scale, 'w2_q': w2_q, 'w2_scale': w2_scale, 'w3_q': w3_q, 'w3_scale': w3_scale}
    _L0_ffn_in = _L0_ffn_setup()
    _L0_c = _w((lambda *s: np.random.randn(*s).astype(np.float32) * 0.05)(4, 1024))
    _L0_wmod = _w((lambda *s: np.random.randn(*s).astype(np.float32) * 0.05)(1024, 6 * 1024) * 1024 ** (-0.5))
    _d = {'L0_attn_data': _L0_attn_in['data'], 'L0_attn_weight': _L0_attn_in['weight'], 'L0_attn_mask': _L0_attn_in['mask'], 'L0_ffn_w1_q': _L0_ffn_in['w1_q'], 'L0_ffn_w1_scale': _L0_ffn_in['w1_scale'], 'L0_ffn_w2_q': _L0_ffn_in['w2_q'], 'L0_ffn_w2_scale': _L0_ffn_in['w2_scale'], 'L0_ffn_w3_q': _L0_ffn_in['w3_q'], 'L0_ffn_w3_scale': _L0_ffn_in['w3_scale'], 'L0_c': _L0_c, 'L0_wmod': _L0_wmod}
    _x0 = _d['L0_attn_data']
    _d['L0_attn_data'] = jax.random.normal(jax.random.fold_in(jax.random.key(seed), 1), (4, 512, 1024), dtype=_x0.dtype)
    del _x0
    return _d

def reference(L0_attn_data, L0_attn_weight, L0_attn_mask, L0_ffn_w1_q, L0_ffn_w1_scale, L0_ffn_w2_q, L0_ffn_w2_scale, L0_ffn_w3_q, L0_ffn_w3_scale, L0_c, L0_wmod):

    def _L0_attn_ref(data, weight, mask):
        import jax, jax.numpy as jnp
        import numpy as np
        BLOCK_H = 32
        BLOCK_W = 32
        N_FEAT = 1024
        K_FEAT = 1024
        N, K = weight.shape
        nb, kb = (N // BLOCK_H, K // BLOCK_W)
        block_mask = mask.reshape(nb, BLOCK_H, kb, BLOCK_W).astype(jnp.float32).sum(axis=(1, 3)) > 0
        elem_mask = jnp.repeat(jnp.repeat(block_mask, BLOCK_H, axis=0), BLOCK_W, axis=1)
        w_masked = weight * elem_mask.astype(weight.dtype)
        out = jnp.einsum('bsk,nk->bsn', data, w_masked)
        return out

    def _L0_ffn_ref(x, w1_q, w1_scale, w2_q, w2_scale, w3_q, w3_scale):
        import jax, jax.numpy as jnp
        import numpy as np
        BLOCK = 64
        NF4_TABLE = jnp.array([-1.0, -0.6961928009986877, -0.5250730514526367, -0.39491748809814453, -0.28444138169288635, -0.18477343022823334, -0.09105003625154495, 0.0, 0.07958029955625534, 0.16093020141124725, 0.24611230194568634, 0.33791524171829224, 0.44070982933044434, 0.5626170039176941, 0.7229568362236023, 1.0], dtype=jnp.float32)
        D_MODEL, HIDDEN = (1024, 2752)
        BATCH, SEQ = (2, 512)

        def dequant_nf4(q, scale):
            O, I = q.shape
            vals = NF4_TABLE[q]
            vals = vals.reshape(O, I // BLOCK, BLOCK) * scale[:, :, None]
            return vals.reshape(O, I)
        w1 = dequant_nf4(w1_q, w1_scale)
        w2 = dequant_nf4(w2_q, w2_scale)
        w3 = dequant_nf4(w3_q, w3_scale)
        h = jax.nn.silu(jnp.einsum('bsd,hd->bsh', x, w1)) * jnp.einsum('bsd,hd->bsh', x, w2)
        return jnp.einsum('bsh,dh->bsd', h, w3)
    x = L0_attn_data
    mod = (_silu(L0_c) @ L0_wmod).reshape(L0_c.shape[0], 6, 1, -1)
    sa, ca, ga, sb, cb, gb = (mod[:, 0], mod[:, 1], mod[:, 2], mod[:, 3], mod[:, 4], mod[:, 5])
    ga = (2 * (ga >= 0) - 1) * jnp.maximum(jnp.abs(ga), 0.25)
    gb = (2 * (gb >= 0) - 1) * jnp.maximum(jnp.abs(gb), 0.25)
    h = _layernorm(x, axis=-1) * (1 + ca) + sa
    x = x + ga * _L0_attn_ref(h, L0_attn_weight, L0_attn_mask)
    h = _layernorm(x, axis=-1) * (1 + cb) + sb
    x = x + gb * _L0_ffn_ref(h, L0_ffn_w1_q, L0_ffn_w1_scale, L0_ffn_w2_q, L0_ffn_w2_scale, L0_ffn_w3_q, L0_ffn_w3_scale)
    return x

_drawn_inputs = setup_inputs


def setup_inputs(seed=0):
    import zlib

    import numpy as np

    out = dict(_drawn_inputs(seed))
    spreads = {}
    factors = {'L0_ffn_w1_scale': 8.0, 'L0_ffn_w2_scale': 8.0, 'L0_ffn_w3_scale': 8.0}
    for name, (base, spread) in spreads.items():
        noise = np.random.default_rng([zlib.crc32(name.encode()), seed]).standard_normal(out[name].shape)
        drawn = base * np.exp(spread * noise) if base else spread * noise
        out[name] = jnp.asarray(drawn.astype(out[name].dtype))
    for name, factor in factors.items():
        out[name] = (out[name] * factor).astype(out[name].dtype)
    return out
```

```python
import numpy as np
import concourse.bass as bass
from concourse import mybir

F32, F32R, I32 = mybir.dt.float32, mybir.dt.float32r, mybir.dt.int32
ALU, ACT, AXL = mybir.AluOpType, mybir.ActivationFunctionType, mybir.AxisListType

P = 128
BATCH, SEQ, D, HID = 4, 512, 1024, 2752
TOK = BATCH * SEQ
TILES = TOK // P
TPB = SEQ // P
C = D // P
NF4B = 64
FULL = HID // P
CH = FULL + 1
PAIRS = FULL // 2 - 1
TAIL = HID - FULL * P
HALF = 512
MASK_B = 32
EPS = 1e-5
KB = 1024

NF4 = [-1.0, -0.6961928009986877, -0.5250730514526367, -0.39491748809814453, -0.28444138169288635,
       -0.18477343022823334, -0.09105003625154495, 0.0, 0.07958029955625534, 0.16093020141124725,
       0.24611230194568634, 0.33791524171829224, 0.44070982933044434, 0.5626170039176941, 0.7229568362236023, 1.0]


def nf4_lines():
    table = np.array(NF4, np.float32).astype(np.float64)
    lines = []
    for q in range(0, 16, 2):
        best = None
        slope = np.float32(table[q + 1] - table[q])
        for da in range(-40, 41):
            a = np.float32(slope + da * np.spacing(slope))
            offset = np.float32(table[q] - np.float64(a) * q)
            for db in (-1, 0, 1):
                b = np.float32(offset + db * np.spacing(offset))
                got = [float(np.float32(np.float64(a) * k + np.float64(b))) for k in (q, q + 1)]
                off = [abs(got[0] - table[q]), abs(got[1] - table[q + 1])]
                if q == 6:
                    off[1] = 0.0 if got[1] >= 0 else 1.0
                key = (max(off), sum(off), abs(da))
                if best is None or key < best[0]:
                    best = (key, float(a), float(b))
        lines.append(best[1:])
    return lines


LINES = nf4_lines()
NL = len(LINES)
READ_BY = [0, 0, 1, 2, 3, 3, 4, 5]
LSLOTS = 3
CSTEPS = 8


def adaln_kernel(nc, cT, x, w12q, w12s, w3q, w3s, wT, maskT, wmod, out):
    base = (nc.sbuf_base + 31) // 32 * 32

    def at(name, shape, dt, kb):
        return nc.alloc_sbuf_tensor_at(name, [P] + shape, dt, offset=base + int(kb * KB))

    HH = at("ffn_in_hi", [BATCH, C, SEQ], F32R, 0)
    HL = at("ffn_in_lo", [BATCH, C, SEQ], F32R, 64)
    WH = at("attn_w_hi", [C, D], F32R, 32)
    WL = at("attn_w_lo", [C, D], F32R, 96)
    WM = [at(f"wmod_{i}", [C // 2, D], F32, kb) for i, kb in enumerate((0, 16, 64))]
    MP = [at(f"mask_piece_{i}", [2, D], I32, kb) for i, kb in enumerate((80, 88))]
    WP = [at(f"weight_piece_{i}", [2, D], F32, kb) for i, kb in enumerate((80, 88))]
    RH = [at(f"w12_hi_{i}", [C, P], F32R, 128 + 4 * i) for i in range(4)]
    RL = [at(f"w12_lo_{i}", [C, P], F32R, 144 + 4 * i) for i in range(4)]
    AH = [at(f"attn_in_hi_{i}", [C, P], F32R, 136 + 4 * i) for i in range(2)]
    AL = [at(f"attn_in_lo_{i}", [C, P], F32R, 152 + 4 * i) for i in range(2)]
    ST = 160
    Q = [at(f"codes_{i}", [C * P], I32, ST + 4 * i) for i in range(2)]
    ACC = [at(f"decoded_{i}", [C * P], F32, ST + 8 + 4 * i) for i in range(2)]
    POS = at("positive_part", [C * P], F32, ST + 16)
    L = [at(f"line_{i}", [C * P], F32, ST + 20 + 4 * i) for i in range(LSLOTS)]
    S12 = [at(f"w12_scale_{i}", [P], F32, ST + 32 + 0.5 * i) for i in range(2)]
    S3 = at("w3_scale", [D], F32, ST + 33)
    SG = at("silu_g", [HALF], F32, ST + 37)
    HT = [at(f"h_tile_{i}", [HALF], F32, ST + 39 + 2 * i) for i in range(2)]
    X = [at(f"x_{i}", [D], F32, ST + 4 * i) for i in range(4)]
    XN = [at(f"normed_{i}", [D], F32, ST + 16 + 4 * i) for i in range(2)]
    HM = [at(f"modulated_{i}", [C, P], F32, ST + 24 + 4 * i) for i in range(2)]
    GA = at("attn_gate", [D], F32, ST + 33)
    XN2 = at("normed_again", [D], F32, ST + 37)
    SGN = at("gate_sign", [D], F32, ST + 37)
    MAG = at("gate", [D], F32, ST + 33)
    W3H = at("w3_hi", [CH, D], F32R, 0)
    W3L = at("w3_lo", [CH, D], F32R, 88)
    DN = 176
    HR = [at(f"h_raw_{i}", [HALF], F32, DN + 2 * i) for i in range(2)]
    HHI = [at(f"h_hi_{i}", [HALF], F32R, DN + 4 + 2 * i) for i in range(2)]
    HLO = [at(f"h_lo_{i}", [HALF], F32R, DN + 8 + 2 * i) for i in range(2)]
    GB = at("ffn_gate", [D], F32, DN + 12)
    YG = at("gated", [D], F32, DN + 16)
    X2 = [at(f"x2_{i}", [D], F32, DN + 20 + 4 * i) for i in range(2)]
    W3R = [at(f"w3_raw_{i}", [D], F32, DN + kb) for i, kb in enumerate((16, 20))]
    free = [ST + 43]

    def small(name, shape, dt=F32):
        t = at(name, shape, dt, free[0])
        free[0] += (int(np.prod(shape)) * 4 + 31) // 32 * 32 / KB
        return t

    IDENT = small("identity", [P])
    GROUP = small("four_partition_groups", [P])
    CT, SC = small("c", [C, BATCH]), small("silu_c", [C, BATCH])
    MODS = [small(f"mod_{i}", [BATCH, 2 * C]) for i in range(2)]
    CUR = [small(f"mod_now_{i}", [2 * C]) for i in range(2)]
    MSUM, MCOL, BMASK = small("mask_sums", [C, D // MASK_B]), small("mask_column", [D // MASK_B]), small("block_mask", [D // MASK_B])
    STATS = [[small(f"stats_{k}{i}", [12]) for i in range(2)] for k in range(2)]
    MV = [[small(f"mean_var_{k}{i}", [2]) for i in range(2)] for k in range(2)]
    VE = [[small(f"var_eps_{k}{i}", [1]) for i in range(2)] for k in range(2)]
    SD = [[small(f"std_{k}{i}", [1]) for i in range(2)] for k in range(2)]
    RS = [[small(f"rstd_{k}{i}", [1]) for i in range(2)] for k in range(2)]
    T1 = [[small(f"newton_{k}{i}", [1]) for i in range(2)] for k in range(2)]
    T2 = [[small(f"newton_factor_{k}{i}", [1]) for i in range(2)] for k in range(2)]
    RF = [[small(f"rstd_fine_{k}{i}", [1]) for i in range(2)] for k in range(2)]

    ps = nc.alloc_psum_tensor("ps", [P, 8, HALF], F32)

    gates_d = nc.dram_tensor("gates_d", (2, BATCH, D), F32, kind="Internal").ap()
    x2_d = nc.dram_tensor("x2_d", (TOK, D), F32, kind="Internal").ap()
    xn2_d = nc.dram_tensor("xn2_d", (TOK, D), F32, kind="Internal").ap()
    h_d = nc.dram_tensor("h_d", (CH * P, TOK), F32, kind="Internal").ap()
    w3_d = nc.dram_tensor("w3_d", (CH * P, D), F32, kind="Internal").ap()

    sem = nc.alloc_semaphore
    c_loaded, ga_loaded, gb_loaded = sem("c_loaded"), sem("ga_loaded"), sem("gb_loaded")
    gate_stored = sem("gate_stored")
    codes_loaded = [sem(f"codes_loaded_{i}") for i in range(2)]
    s12_loaded = [sem(f"s12_loaded_{i}") for i in range(2)]
    s3_loaded = sem("s3_loaded")
    wmod_loaded = [sem(f"wmod_loaded_{i}") for i in range(3)]
    piece_loaded = [sem(f"piece_loaded_{i}") for i in range(2)]
    x_loaded = [sem(f"x_loaded_{i}") for i in range(4)]
    x2_stored = [sem(f"x2_stored_{i}") for i in range(4)]
    xn2_stored = sem("xn2_stored")
    xn2_loaded = [sem(f"xn2_loaded_{i}") for i in range(4)]
    h_stored = [sem(f"h_stored_{i}") for i in range(2)]
    w3_stored = sem("w3_stored")
    h_loaded = [sem(f"h_loaded_{i}") for i in range(2)]
    w3_loaded = [sem(f"w3_loaded_{i}") for i in range(2)]
    x2_loaded = [sem(f"x2_loaded_{i}") for i in range(2)]
    out_stored = [sem(f"out_stored_{i}") for i in range(2)]
    consts_made = sem("consts_made")
    pool_step = sem("pool_step")
    silu_c_made = sem("silu_c_made")
    wmod_used = sem("wmod_used")
    mod_read = sem("mod_read")
    gate_step = sem("gate_step")
    mask_step = sem("mask_step")
    mask_summed = sem("mask_summed")
    piece_masked = sem("piece_masked")
    w_hi = sem("w_hi")
    w_lo = sem("w_lo")
    line_ready = sem("line_ready")
    combined = sem("combined")
    w12_hi = sem("w12_hi")
    w12_lo = sem("w12_lo")
    ln_step = sem("ln_step")
    sqrt_done = sem("sqrt_done")
    mod_now = sem("mod_now")
    turned = sem("turned")
    modulated = sem("modulated")
    tile_hi = sem("tile_hi")
    tile_lo = sem("tile_lo")
    attn_done = sem("attn_done")
    gated = sem("gated")
    x2_made = sem("x2_made")
    stage_done = sem("stage_done")
    up_done = sem("up_done")
    silu_done = sem("silu_done")
    h_made = sem("h_made")
    h_hi, h_lo = sem("h_hi"), sem("h_lo")
    w3_hi, w3_lo = sem("w3_hi"), sem("w3_lo")
    h_used = sem("h_used")
    y_gated = sem("y_gated")
    out_made = sem("out_made")

    MOD_BANK, MASK_BANK = {0: 0, 1: 3, 3: 4, 4: 5}, 6
    LN_STEPS, GATE_STEPS = 9, 5

    def ln_index(kind, t):
        if kind == 0:
            return t if isinstance(t, int) and t < 2 else 2 * t - 2
        return {14: 30, 15: 31}.get(t, None) or 2 * t + 3 if isinstance(t, int) else 2 * t + 3

    def first_n(c):
        return 2 + 3 * c

    def tiles_of(c):
        if isinstance(c, int) and c == FULL:
            return [2]
        if isinstance(c, int) and c == FULL - 1:
            return [0, 2]
        return [0, 1, 2]

    def number(c, kind):
        if isinstance(c, int) and c == FULL:
            return first_n(FULL - 1) + 2
        if isinstance(c, int) and c == FULL - 1 and kind == 2:
            return first_n(c) + 1
        return first_n(c) + kind

    block = nc.Block()
    with block:

        @block.sync
        def _(sp):
            sp.dma_start(CT[:], cT.rearrange("p (c b) -> p c b", b=BATCH)).then_inc(c_loaded, 16)
            wmod_v = wmod.rearrange("(p c) f -> p c f", c=C)

            def load_wmod(j):
                if j >= 3:
                    sp.wait_ge(wmod_used, j - 2)
                m, half = j // 2, j % 2
                sp.dma_start(WM[j % 3][:], wmod_v[:, 4 * half:4 * half + 4, m * D:(m + 1) * D]).then_inc(wmod_loaded[j % 3], 16)

            def load_codes(n, src, slot):
                sp.dma_start(Q[slot][0:src.shape[0], :], src).then_inc(codes_loaded[slot], 16)

            def load_s12(tile, w):
                src = w12s[tile].unsqueeze(1).broadcast_to([P // 8, 8, P])
                sp.dma_start(S12[w][:], src).then_inc(s12_loaded[w], 16)

            for w in range(2):
                load_codes(w, w12q[w], w)
                load_s12(w, w)
            for j in range(4):
                load_wmod(j)
            for t in range(4):
                sp.wait_ge(w12_lo, 2)
                sp.dma_start(X[t][:], x[t * P:(t + 1) * P, :]).then_inc(x_loaded[t], 16)
            for j in range(4, 6):
                load_wmod(j)
            sp.wait_ge(gate_step, GATE_STEPS)
            sp.dma_start(gates_d[0], MAG[0:BATCH, :]).then_inc(gate_stored, 16)
            for j in range(6, 12):
                load_wmod(j)
            sp.wait_ge(gate_step, 2 * GATE_STEPS)
            sp.dma_start(gates_d[1], MAG[0:BATCH, :]).then_inc(gate_stored, 16)
            sp.wait_ge(gate_stored, 32)
            sp.dma_start(GA[:], gates_d[0, 0].partition_broadcast(P)).then_inc(ga_loaded, 16)

            def attn_io(b, k, more, gate):
                t = TPB * b + k
                sp.wait_ge(x2_made, t + 1)
                sp.dma_start(x2_d[bass.ds(t * P, P), :], X[k][:]).then_inc(x2_stored[k], 16)
                if gate:
                    sp.dma_start(GA[:], gates_d[0, b + 1].partition_broadcast(P)).then_inc(ga_loaded, 16)
                if isinstance(t, int) and t == TILES - 1:
                    sp.wait_ge(ln_step, LN_STEPS * TILES * 2)
                elif isinstance(t, int) and t == TILES - 2:
                    sp.wait_ge(ln_step, LN_STEPS * (TILES * 2 - 1))
                else:
                    sp.wait_ge(ln_step, LN_STEPS * (2 * t + 4))
                sp.dma_start(xn2_d[bass.ds(t * P, P), :], XN2[:]).then_inc(xn2_stored, 16)
                if more:
                    sp.wait_ge(x2_stored[k], 16 * (b + 1))
                    sp.dma_start(X[k][:], x[bass.ds((t + TPB) * P, P), :]).then_inc(x_loaded[k], 16)

            with sp.Fori(0, BATCH - 1) as b:
                for k in range(TPB):
                    attn_io(b, k, True, k == TPB - 1)
            for k in range(TPB):
                attn_io(BATCH - 1, k, False, False)

            def ln2_io(b, k):
                t = TPB * b + k
                if isinstance(b, int):
                    sp.wait_ge(x2_stored[k], 16 * BATCH)
                    if k == 0:
                        sp.wait_ge(xn2_stored, 16 * TILES)
                else:
                    sp.wait_ge(turned, TILES + t - TPB + 1)
                sp.dma_start(X[k][:], xn2_d[bass.ds(t * P, P), :]).then_inc(xn2_loaded[k], 16)

            for k in range(TPB):
                ln2_io(0, k)
            with sp.Fori(1, BATCH) as b:
                for k in range(TPB):
                    ln2_io(b, k)

            def fetch(n, c, kind):
                slot = (n if isinstance(n, int) else n_par[kind]) % 2
                if kind == 2:
                    rows = TAIL if isinstance(c, int) and c == CH - 1 else P
                    load_codes(n, w3q[bass.ds(c * P, rows), :], slot)
                    for g in range(rows // NF4B):
                        sp.dma_start(S3[g * NF4B:(g + 1) * NF4B, :],
                                     w3s[2 * c + g].partition_broadcast(NF4B)).then_inc(s3_loaded, 16)
                else:
                    load_codes(n, w12q[2 * c + 2 + kind], slot)
                    load_s12(2 * c + 2 + kind, kind)

            n_par = [0, 0, 0]

            def fetch_after(c, kind, par):
                n = number(c, kind)
                n_par[kind] = par
                if kind == 2 and isinstance(c, int) and c >= FULL - 1:
                    sp.wait_ge(combined, CSTEPS * (number(c - 1, 2) + 1))
                else:
                    sp.wait_ge(combined, CSTEPS * (n - 2))
                sp.wait_ge(line_ready, NL * (n - 1))
                fetch(n, c, kind)

            def store_h(c, b):
                sp.wait_ge(h_made, TPB * (c + 1) + b + 1)
                rows = TAIL if isinstance(c, int) and c == FULL else P
                sp.dma_start(h_d[bass.ds(c * P, rows), b * HALF:(b + 1) * HALF],
                             HT[b % 2][0:rows, :]).then_inc(h_stored[b % 2], 16)

            def store_w3(c, par):
                n = number(c, 2)
                sp.wait_ge(combined, CSTEPS * (n + 1))
                rows = TAIL if isinstance(c, int) and c == FULL else P
                sp.dma_start(w3_d[bass.ds(c * P, rows), :], ACC[par][0:rows, :]).then_inc(w3_stored, 16)

            def up_io(c, cpar):
                seq = tiles_of(c)
                par = {kind: (cpar + i) % 2 for i, kind in enumerate(seq)}
                if seq == [2]:
                    par = {2: (first_n(FULL - 1) + 2) % 2}
                nxt = c + 1
                last = isinstance(c, int) and c == FULL
                nseq = [] if last else tiles_of(nxt)
                if seq[-1] == 2 and len(seq) == 3:
                    fetch_after(c, 2, par[2])
                store_h(c, 0)
                npar = {kind: (cpar + 1 + i) % 2 for i, kind in enumerate(nseq)}
                if nseq == [2]:
                    npar = {2: (first_n(FULL - 1) + 2) % 2}
                if nseq:
                    fetch_after(nxt, nseq[0], npar[nseq[0]])
                store_h(c, 1)
                if len(nseq) > 1:
                    fetch_after(nxt, nseq[1], npar[nseq[1]])
                store_w3(c, par[2])
                store_h(c, 2)
                store_h(c, 3)

            sp.wait_ge(tile_lo, 2 * TILES)
            for kind in range(2):
                n_par[kind] = kind
                fetch(first_n(0) + kind, 0, kind)
            up_io(0, 0)
            up_io(1, 1)
            with sp.Fori(1, PAIRS) as i:
                up_io(2 * i, 0)
                up_io(2 * i + 1, 1)
            for c in range(2 * PAIRS, FULL):
                up_io(c, c % 2)
            up_io(FULL, FULL % 2)

            sp.wait_ge(stage_done, 1 + CH)
            for s in range(2):
                sp.wait_ge(h_stored[s], 16 * CH * TPB // 2)
            sp.wait_ge(w3_stored, 16 * CH)

            def load_h(tb, ch, par):
                rows = TAIL if isinstance(ch, int) and ch == CH - 1 else P
                g = tb * CH + ch
                if not (isinstance(tb, int) and tb == 0 and isinstance(ch, int) and ch < 2):
                    sp.wait_ge(h_lo, g - 1)
                sp.dma_start(HR[par][0:rows, :], h_d[bass.ds(ch * P, rows), bass.ds(tb * HALF, HALF)])\
                  .then_inc(h_loaded[par], 16)

            def load_w3(ch, par):
                rows = TAIL if isinstance(ch, int) and ch == CH - 1 else P
                if not (isinstance(ch, int) and ch < 2):
                    sp.wait_ge(w3_lo, ch - 1)
                sp.dma_start(W3R[par][0:rows, :], w3_d[bass.ds(ch * P, rows), :]).then_inc(w3_loaded[par], 16)

            def store_out(tb, k):
                t = tb * TPB + k
                sp.wait_ge(out_made, t + 1)
                sp.dma_start(out[bass.ds(t * P, P), :], X2[k % 2][:]).then_inc(out_stored[k % 2], 16)

            def block_out(tb):
                if isinstance(tb, int) and tb == 0:
                    sp.wait_ge(w3_lo, CH)
                else:
                    sp.wait_ge(y_gated, tb * TPB)
                sp.dma_start(GB[:], gates_d[1, tb].partition_broadcast(P)).then_inc(gb_loaded, 16)
                for k in range(TPB):
                    if k >= 2 or not (isinstance(tb, int) and tb == 0):
                        sp.wait_ge(out_stored[k % 2], 16 * (tb * (TPB // 2) + k // 2))
                    sp.dma_start(X2[k % 2][:], x2_d[bass.ds((tb * TPB + k) * P, P), :]).then_inc(x2_loaded[k % 2], 16)
                    if k >= 1:
                        store_out(tb, k - 1)
                store_out(tb, TPB - 1)

            def down_io(tb, with_w3, more):
                with sp.Fori(1, CH // 2 - 1) as i:
                    for k in range(2):
                        load_h(tb, 2 * i + k, k)
                        if with_w3:
                            load_w3(2 * i + k, k)
                for ch in range(CH - 2, CH):
                    load_h(tb, ch, ch % 2)
                    if with_w3:
                        load_w3(ch, ch % 2)
                if more:
                    for ch in range(2):
                        load_h(tb + 1, ch, ch)
                block_out(tb)

            for ch in range(2):
                load_h(0, ch, ch)
                load_w3(ch, ch)
            down_io(0, True, True)
            with sp.Fori(1, BATCH - 1) as tb:
                down_io(tb, False, True)
            down_io(BATCH - 1, False, False)
            for s in range(2):
                sp.wait_ge(out_stored[s], 16 * TILES // 2)

        @block.gpsimd
        def _(pool):
            pool.memset(IDENT[:], 0.0).then_inc(pool_step, 1)
            pool.memset(GROUP[:], 1.0).then_inc(pool_step, 1)
            pool.wait_ge(pool_step, 2)
            pool.affine_select(out=IDENT[:], in_=IDENT[:], compare_op=ALU.not_equal, fill=1.0, base=0,
                               pattern=[[-1, P]], channel_multiplier=1).then_inc(consts_made, 1)
            g3 = GROUP[:].rearrange("p (g o) -> p g o", o=4)
            pool.affine_select(out=g3, in_=g3, compare_op=ALU.is_ge, fill=0.0, base=0,
                               pattern=[[-4, P // 4], [0, 4]], channel_multiplier=1).then_inc(pool_step, 1)
            pool.wait_ge(pool_step, 3)
            pool.affine_select(out=g3, in_=g3, compare_op=ALU.is_ge, fill=0.0, base=3,
                               pattern=[[4, P // 4], [0, 4]], channel_multiplier=-1).then_inc(consts_made, 1)
            mask_v = maskT.rearrange("(p c) n -> p c n", c=C)
            w_v = wT.rearrange("(p c) n -> p c n", c=C)
            for j in range(8):
                if j >= 2:
                    if j - 2 < 4:
                        pool.wait_ge(mask_step, j - 1)
                    else:
                        pool.wait_ge(w_lo, j - 5)
                if j < 4:
                    pool.dma_start(MP[j % 2][:], mask_v[:, 2 * j:2 * j + 2, :]).then_inc(piece_loaded[j % 2], 16)
                else:
                    i = j - 4
                    pool.dma_start(WP[j % 2][:], w_v[:, 2 * i:2 * i + 2, :]).then_inc(piece_loaded[j % 2], 16)

        def line_free(eng, n, j):
            if j >= LSLOTS:
                eng.wait_ge(combined, CSTEPS * n + READ_BY[j - LSLOTS] + 1)
            elif not (isinstance(n, int) and n == 0):
                eng.wait_ge(combined, CSTEPS * (n - 1) + READ_BY[j - LSLOTS + NL] + 1)

        @block.scalar
        def _(act):
            act.wait_ge(c_loaded, 16)
            act.activation(SC[:], CT[:], ACT.Silu).then_inc(silu_c_made, 1)

            def lines(n, npar, first_line, codes_wait, rows=P):
                act.wait_ge(codes_loaded[npar], codes_wait)
                for j, (slope, offset) in enumerate(LINES):
                    line_free(act, n, j)
                    act.activation(L[(first_line + j) % LSLOTS][0:rows, :], Q[npar][0:rows, :], ACT.Copy,
                                   bias=offset, scale=slope).then_inc(line_ready, 1)

            def w12_high(n, npar, ring):
                act.wait_ge(combined, CSTEPS * (n + 1))
                act.activation(RH[ring][:], ACC[npar][:].rearrange("p (c h) -> p c h", c=C), ACT.Copy).then_inc(w12_hi, 1)

            for n in range(2):
                lines(n, n, NL * n, 16)
            for n in range(2):
                w12_high(n, n, n)
            for j in range(4):
                act.wait_ge(piece_masked, j + 1)
                act.activation(WH[:, 2 * j:2 * j + 2, :], WP[j % 2][:], ACT.Copy).then_inc(w_hi, 1)

            def root(kind, t, k):
                i = ln_index(kind, t)
                act.wait_ge(ln_step, LN_STEPS * i + 4)
                act.activation(SD[kind][k][:], VE[kind][k][:], ACT.Sqrt).then_inc(sqrt_done, 1)

            def mod_for(ln, b, count):
                act.activation(CUR[ln][:], MODS[ln][:, b, :], ACT.Copy).then_inc(mod_now, 1)
                act.wait_ge(mod_now, count + 1)

            def modulate(u, par, ln, first):
                act.wait_ge(turned, u + 1)
                if not first:
                    act.wait_ge(tile_lo, u - 1)
                for c in range(C):
                    ins = act.activation(HM[par][:, c, :], ps[:, 4 + 2 * par + c // 4, (c % 4) * P:(c % 4 + 1) * P],
                                         ACT.Identity, bias=CUR[ln][:, c:c + 1], scale=CUR[ln][:, C + c:C + c + 1])
                ins.then_inc(modulated, 1)
                act.wait_ge(modulated, u + 1)

            def attn_high(t, par, first):
                if not first:
                    act.wait_ge(attn_done, t - 1)
                act.activation(AH[par][:], HM[par][:], ACT.Copy).then_inc(tile_hi, 1)

            act.wait_ge(mod_read, 2)
            root(0, 0, 0)
            root(0, 1, 1)
            mod_for(0, 0, 0)
            modulate(0, 0, 0, True)
            attn_high(0, 0, True)

            def attn_step(b, k, has_next, has_prev, has_load):
                t = TPB * b + k
                if has_next:
                    if k == TPB - 1:
                        mod_for(0, b + 1, b + 1)
                    first = isinstance(t, int) and t == 0
                    modulate(t + 1, (k + 1) % 2, 0, first)
                    attn_high(t + 1, (k + 1) % 2, first)
                if has_prev:
                    root(1, t - 1, (k + 1) % 2)
                if has_load:
                    root(0, t + 2, k % 2)

            for k in range(TPB):
                attn_step(0, k, True, k > 0, True)
            with act.Fori(1, BATCH - 1) as b:
                for k in range(TPB):
                    attn_step(b, k, True, True, True)
            for k in range(TPB):
                attn_step(BATCH - 1, k, k < TPB - 1, True, k < TPB - 2)
            root(1, TILES - 1, 1)

            act.wait_ge(mod_read, 4)
            with act.Fori(0, BATCH) as b:
                mod_for(1, b, BATCH + b)
                for k in range(TPB):
                    t = TPB * b + k
                    modulate(TILES + t, k % 2, 1, False)
                    act.activation(HH[:, b, :, k * P:(k + 1) * P], HM[k % 2][:], ACT.Copy).then_inc(tile_hi, 1)

            def silu(c, b, rows=P):
                act.wait_ge(up_done, TPB * c + b + 1)
                if not (isinstance(c, int) and c == 0 and b == 0):
                    act.wait_ge(h_made, TPB * (c + 1) + b)
                act.activation(SG[0:rows, :], ps[0:rows, 2 * b, :], ACT.Silu).then_inc(silu_done, 1)

            def up_step(c, cpar):
                seq = tiles_of(c)
                for i, kind in enumerate(seq):
                    n = number(c, kind)
                    npar = (cpar + i) % 2 if len(seq) > 1 else n % 2
                    rows = TAIL if seq == [2] else P
                    first = NL * number(c if isinstance(c, int) else cpar, kind)
                    lines(n, npar, first, codes_wait_value(n, npar), rows)
                    if i > 0 and seq[i - 1] != 2:
                        prev = seq[i - 1]
                        act.wait_ge(stage_done, c + 1)
                        w12_high(n - 1, (npar + 1) % 2, 2 * ((cpar + 1) % 2) + prev)
                    silu(c, i)
                for b in range(len(seq), TPB):
                    silu(c, b, TAIL if seq == [2] else P)

            def codes_wait_value(n, npar):
                return 16 * (n // 2 + 1) if isinstance(n, int) else 8 * (n - npar) + 16

            up_step(0, 0)
            up_step(1, 1)
            with act.Fori(1, PAIRS) as i:
                up_step(2 * i, 0)
                up_step(2 * i + 1, 1)
            for c in range(2 * PAIRS, FULL):
                up_step(c, c % 2)
            c = FULL
            n = number(c, 2)
            lines(n, n % 2, NL * n, codes_wait_value(n, n % 2), TAIL)
            for b in range(TPB):
                silu(c, b, TAIL)

            def high(tb, ch, par, with_w3):
                rows = TAIL if isinstance(ch, int) and ch == CH - 1 else P
                g = tb * CH + ch
                count = 16 * (tb * (CH // 2) + ch // 2 + 1) if isinstance(ch, int) else 16 * (tb * (CH // 2)) + 8 * (ch - par) + 16
                act.wait_ge(h_loaded[par], count)
                if not (isinstance(g, int) and g < 2):
                    act.wait_ge(h_used, g - 1)
                act.activation(HHI[par][0:rows, :], HR[par][0:rows, :], ACT.Copy).then_inc(h_hi, 1)
                if with_w3:
                    act.wait_ge(w3_loaded[par], count)
                    act.activation(W3H[0:rows, ch, :], W3R[par][0:rows, :], ACT.Copy).then_inc(w3_hi, 1)

            def down_high(tb, with_w3):
                for ch in range(2):
                    high(tb, ch, ch, with_w3)
                with act.Fori(1, CH // 2 - 1) as i:
                    for k in range(2):
                        high(tb, 2 * i + k, k, with_w3)
                for ch in range(CH - 2, CH):
                    high(tb, ch, ch % 2, with_w3)

            act.wait_ge(stage_done, 1 + CH)
            down_high(0, True)
            with act.Fori(1, BATCH) as tb:
                down_high(tb, False)

        @block.vector
        def _(dve):
            def combine(n, npar, first_line, scale, scale_sem, scale_count, rows=P):
                acc, pos = ACC[npar][0:rows, :], POS[0:rows, :]

                def line(j):
                    return L[(first_line + j) % LSLOTS][0:rows, :]

                def step(k, j):
                    dve.wait_ge(line_ready, NL * n + j + 1)
                    if not (isinstance(n, int) and n == 0 and k == 0):
                        dve.wait_ge(combined, CSTEPS * n + k)

                step(0, 1)
                dve.tensor_tensor(acc, line(0), line(1), ALU.min).then_inc(combined, 1)
                step(1, 2)
                dve.scalar_tensor_tensor(out=acc, in0=line(2), scalar=0.0, in1=acc, op0=ALU.min, op1=ALU.min).then_inc(combined, 1)
                step(2, 3)
                dve.tensor_tensor(acc, line(3), acc, ALU.min).then_inc(combined, 1)
                step(3, 5)
                dve.scalar_tensor_tensor(out=pos, in0=line(4), scalar=0.0, in1=line(5), op0=ALU.max, op1=ALU.max).then_inc(combined, 1)
                step(4, 6)
                dve.tensor_tensor(pos, line(6), pos, ALU.max).then_inc(combined, 1)
                step(5, 7)
                dve.tensor_tensor(pos, line(7), pos, ALU.max).then_inc(combined, 1)
                step(6, 7)
                dve.tensor_tensor(acc, acc, pos, ALU.add).then_inc(combined, 1)
                step(7, 7)
                dve.wait_ge(scale_sem, scale_count)
                if scale.shape[1] == P:
                    acc3 = acc.rearrange("p (c h) -> p c h", c=C)
                    dve.tensor_tensor(acc3, acc3, scale.unsqueeze(1).broadcast_to([P, C, P]), ALU.mult).then_inc(combined, 1)
                else:
                    dve.tensor_tensor(acc, acc, scale, ALU.mult).then_inc(combined, 1)

            def w12_low(n, npar, ring, count):
                dve.wait_ge(w12_hi, count)
                dve.wait_ge(combined, CSTEPS * (n + 1))
                dve.tensor_tensor(RL[ring][:], ACC[npar][:].rearrange("p (c h) -> p c h", c=C),
                                  RH[ring][:].bitcast(F32), ALU.subtract).then_inc(w12_lo, 1)

            for n in range(2):
                combine(n, n, NL * n, S12[n][:], s12_loaded[n], 16)
            for n in range(2):
                w12_low(n, n, n, n + 1)

            for j in range(4):
                dve.wait_ge(piece_loaded[j % 2], 16 * (j // 2 + 1))
                dve.tensor_reduce(MSUM[:, 2 * j:2 * j + 2, :], MP[j % 2][:].rearrange("p c (n o) -> p c n o", o=MASK_B),
                                  AXL.X, ALU.add).then_inc(mask_step, 1)
            dve.wait_ge(mask_step, 4)
            dve.tensor_reduce(MCOL[:], MSUM[:].rearrange("p c n -> p n c"), AXL.X, ALU.add).then_inc(mask_step, 1)
            dve.wait_ge(mask_summed, 1)
            dve.tensor_scalar(BMASK[:], ps[:, MASK_BANK, 0:D // MASK_B], 0.0, None, ALU.is_gt).then_inc(mask_step, 1)
            dve.wait_ge(mask_step, 6)
            for j in range(4):
                dve.wait_ge(piece_loaded[j % 2], 16 * (j // 2 + 3))
                w4 = WP[j % 2][:].rearrange("p c (n o) -> p c n o", o=MASK_B)
                dve.tensor_tensor(w4, w4, BMASK[:].unsqueeze(1).unsqueeze(3).broadcast_to([P, 2, D // MASK_B, MASK_B]),
                                  ALU.mult).then_inc(piece_masked, 1)
                dve.wait_ge(w_hi, j + 1)
                dve.tensor_tensor(WL[:, 2 * j:2 * j + 2, :], WP[j % 2][:], WH[:, 2 * j:2 * j + 2, :].bitcast(F32),
                                  ALU.subtract).then_inc(w_lo, 1)

            for m in range(6):
                dve.wait_ge(wmod_used, 2 * (m + 1))
                if m % 3 < 2:
                    ln, s = m // 3, m % 3
                    src = ps[:, MOD_BANK[m], 0:C * BATCH].rearrange("p (c b) -> p b c", b=BATCH)
                    dve.tensor_scalar(MODS[ln][:, :, s * C:(s + 1) * C], src, float(s), None, ALU.add).then_inc(mod_read, 1)
                else:
                    g = m // 3
                    src = ps[0:BATCH, 1:3, :].rearrange("p a n -> p (a n)")
                    if g:
                        dve.wait_ge(gate_stored, 16)
                    sgn, mag = SGN[0:BATCH, :], MAG[0:BATCH, :]
                    dve.tensor_scalar(sgn, src, 0.0, 2.0, ALU.is_ge, ALU.mult).then_inc(gate_step, 1)
                    dve.tensor_copy(mag, src).then_inc(gate_step, 1)
                    dve.wait_ge(gate_step, GATE_STEPS * g + 2)
                    dve.scalar_tensor_tensor(out=mag, in0=mag, scalar=-1.0, in1=mag, op0=ALU.mult, op1=ALU.max).then_inc(gate_step, 1)
                    dve.wait_ge(gate_step, GATE_STEPS * g + 3)
                    dve.tensor_scalar(mag, mag, 0.25, None, ALU.max).then_inc(gate_step, 1)
                    dve.wait_ge(gate_step, GATE_STEPS * g + 4)
                    dve.scalar_tensor_tensor(out=mag, in0=sgn, scalar=-1.0, in1=mag, op0=ALU.add, op1=ALU.mult).then_inc(gate_step, 1)

            def layernorm(kind, t, k, src, dst, before):
                i = LN_STEPS * ln_index(kind, t)
                st, mv, ve, sd = STATS[kind][k], MV[kind][k], VE[kind][k], SD[kind][k]
                rs, t1, t2, rf = RS[kind][k], T1[kind][k], T2[kind][k], RF[kind][k]
                dve.bn_stats(st[:, 0:6], src[:, 0:HALF]).then_inc(ln_step, 1)
                dve.bn_stats(st[:, 6:12], src[:, HALF:D]).then_inc(ln_step, 1)
                dve.wait_ge(ln_step, i + 2)
                dve.memset(ve[:], EPS)
                dve.bn_aggr(mv[:], st[:]).then_inc(ln_step, 1)
                dve.wait_ge(ln_step, i + 3)
                dve.tensor_tensor(ve[:], mv[:, 1:2], ve[:], ALU.add).then_inc(ln_step, 1)
                dve.wait_ge(sqrt_done, ln_index(kind, t) + 1)
                dve.reciprocal(rs[:], sd[:]).then_inc(ln_step, 1)
                dve.wait_ge(ln_step, i + 5)
                dve.scalar_tensor_tensor(out=t1[:], in0=rs[:], scalar=ve[:], in1=rs[:], op0=ALU.mult, op1=ALU.mult).then_inc(ln_step, 1)
                dve.wait_ge(ln_step, i + 6)
                dve.tensor_scalar(t2[:], t1[:], -0.5, 1.5, ALU.mult, ALU.add).then_inc(ln_step, 1)
                dve.wait_ge(ln_step, i + 7)
                dve.tensor_tensor(rf[:], rs[:], t2[:], ALU.mult).then_inc(ln_step, 1)
                dve.wait_ge(ln_step, i + 8)
                before()
                dve.tensor_scalar(dst, src, mv[:, 0:1], rf[:], ALU.subtract, ALU.mult).then_inc(ln_step, 1)

            def ln1(b, k):
                t = TPB * b + k
                dve.wait_ge(x_loaded[k], 16 * (b + 1))

                def before():
                    if not (isinstance(t, int) and t < 2):
                        dve.wait_ge(turned, t - 1)
                layernorm(0, t, k % 2, X[k][:], XN[k % 2][:], before)

            def attn_low(t, par):
                dve.wait_ge(tile_hi, t + 1)
                dve.tensor_tensor(AL[par][:], HM[par][:], AH[par][:].bitcast(F32), ALU.subtract).then_inc(tile_lo, 1)

            def residual(b, k):
                t = TPB * b + k
                dve.wait_ge(attn_done, t + 1)
                if k == 0:
                    dve.wait_ge(ga_loaded, 16 * (b + 1))
                if not (isinstance(t, int) and t == 0):
                    dve.wait_ge(xn2_stored, 16 * t)
                attn = ps[:, 2 * (k % 2):2 * (k % 2) + 2, :].rearrange("p a n -> p (a n)")
                dve.tensor_tensor(XN2[:], attn, GA[:], ALU.mult).then_inc(gated, 1)
                dve.wait_ge(gated, t + 1)
                dve.tensor_tensor(X[k][:], X[k][:], XN2[:], ALU.add).then_inc(x2_made, 1)
                dve.wait_ge(x2_made, t + 1)
                layernorm(1, t, k % 2, X[k][:], XN2[:], lambda: None)

            ln1(0, 0)
            ln1(0, 1)
            attn_low(0, 0)

            def attn_step(b, k, has_next, has_prev, has_load):
                t = TPB * b + k
                if has_next:
                    attn_low(t + 1, (k + 1) % 2)
                if has_prev:
                    pb, pk = (b, k - 1) if k else (b - 1, TPB - 1)
                    residual(pb, pk)
                if has_load:
                    lb, lk = (b, k + 2) if k + 2 < TPB else (b + 1, k + 2 - TPB)
                    ln1(lb, lk)

            for k in range(TPB):
                attn_step(0, k, True, k > 0, True)
            with dve.Fori(1, BATCH - 1) as b:
                for k in range(TPB):
                    attn_step(b, k, True, True, True)
            for k in range(TPB):
                attn_step(BATCH - 1, k, k < TPB - 1, True, k < TPB - 2)
            residual(BATCH - 1, TPB - 1)

            with dve.Fori(0, BATCH) as b:
                for k in range(TPB):
                    t = TPB * b + k
                    dve.wait_ge(tile_hi, TILES + t + 1)
                    dve.tensor_tensor(HL[:, b, :, k * P:(k + 1) * P], HM[k % 2][:],
                                      HH[:, b, :, k * P:(k + 1) * P].bitcast(F32), ALU.subtract).then_inc(tile_lo, 1)
            dve.wait_ge(tile_lo, 2 * TILES)
            dve.sem_inc(h_made, TPB)

            def make_h(c, b):
                dve.wait_ge(silu_done, TPB * c + b + 1)
                if isinstance(c, int) and c == 0 and b < 2:
                    pass
                else:
                    dve.wait_ge(h_stored[b % 2], 16 * ((TPB // 2) * c + b // 2))
                if isinstance(c, int) and c == FULL:
                    dve.tensor_tensor(HT[b % 2][0:TAIL, :], SG[0:TAIL, :], ps[TAIL:2 * TAIL, 2 * b, :], ALU.mult).then_inc(h_made, 1)
                else:
                    dve.tensor_tensor(HT[b % 2][:], SG[:], ps[:, 2 * b + 1, :], ALU.mult).then_inc(h_made, 1)

            def up_step(c, cpar):
                seq = tiles_of(c)
                for i, kind in enumerate(seq):
                    n = number(c, kind)
                    npar = (cpar + i) % 2 if len(seq) > 1 else n % 2
                    rows = TAIL if seq == [2] else P
                    first = NL * number(c if isinstance(c, int) else cpar, kind)
                    if kind == 1 and not (isinstance(c, int) and c == 0):
                        dve.wait_ge(w3_stored, 16 * c)
                    if kind == 2 and isinstance(c, int) and c >= FULL - 1:
                        dve.wait_ge(w3_stored, 16 * c)
                    if kind == 0:
                        dve.wait_ge(w12_lo, 2 * c + 2)
                    if kind == 2 and not (isinstance(c, int) and c >= FULL - 1):
                        dve.wait_ge(w12_lo, 2 * c + 3)
                    if kind == 2:
                        loads = 2 * c + 2 if rows == P else 2 * c + 1
                        combine(n, npar, first, S3[0:rows, :], s3_loaded, 16 * loads, rows)
                    else:
                        combine(n, npar, first, S12[kind][:], s12_loaded[kind], 16 * (c + 2))
                    if i > 0 and seq[i - 1] != 2:
                        prev = seq[i - 1]
                        dve.wait_ge(stage_done, c + 1)
                        w12_low(n - 1, (npar + 1) % 2, 2 * ((cpar + 1) % 2) + prev, 2 * c + 3 + prev)
                    make_h(c, i)
                for b in range(len(seq), TPB):
                    make_h(c, b)

            up_step(0, 0)
            up_step(1, 1)
            with dve.Fori(1, PAIRS) as i:
                up_step(2 * i, 0)
                up_step(2 * i + 1, 1)
            for c in range(2 * PAIRS, FULL):
                up_step(c, c % 2)
            c = FULL
            n = number(c, 2)
            dve.wait_ge(w3_stored, 16 * c)
            dve.wait_ge(w12_lo, 2 * FULL + 1)
            combine(n, n % 2, NL * n, S3[0:TAIL, :], s3_loaded, 16 * (2 * c + 1), TAIL)
            for b in range(TPB):
                make_h(c, b)

            def low(tb, ch, par, with_w3):
                rows = TAIL if isinstance(ch, int) and ch == CH - 1 else P
                g = tb * CH + ch
                dve.wait_ge(h_hi, g + 1)
                if not (isinstance(g, int) and g < 2):
                    dve.wait_ge(h_used, g - 1)
                dve.tensor_tensor(HLO[par][0:rows, :], HR[par][0:rows, :], HHI[par][0:rows, :].bitcast(F32),
                                  ALU.subtract).then_inc(h_lo, 1)
                if with_w3:
                    dve.wait_ge(w3_hi, ch + 1)
                    dve.tensor_tensor(W3L[0:rows, ch, :], W3R[par][0:rows, :], W3H[0:rows, ch, :].bitcast(F32),
                                      ALU.subtract).then_inc(w3_lo, 1)

            def down_low(tb, with_w3):
                for ch in range(2):
                    low(tb, ch, ch, with_w3)
                with dve.Fori(1, CH // 2 - 1) as i:
                    for k in range(2):
                        low(tb, 2 * i + k, k, with_w3)
                for ch in range(CH - 2, CH):
                    low(tb, ch, ch % 2, with_w3)
                dve.wait_ge(gb_loaded, 16 * (tb + 1))
                dve.wait_ge(h_used, CH * (tb + 1))
                for k in range(TPB):
                    t = TPB * tb + k
                    y = ps[:, 2 * k:2 * k + 2, :].rearrange("p a n -> p (a n)")
                    if not (isinstance(t, int) and t == 0):
                        dve.wait_ge(out_made, t)
                    dve.tensor_tensor(YG[:], y, GB[:], ALU.mult).then_inc(y_gated, 1)
                    dve.wait_ge(y_gated, t + 1)
                    dve.wait_ge(x2_loaded[k % 2], 16 * (2 * tb + k // 2 + 1))
                    dve.tensor_tensor(X2[k % 2][:], X2[k % 2][:], YG[:], ALU.add).then_inc(out_made, 1)

            dve.wait_ge(stage_done, 1 + CH)
            down_low(0, True)
            with dve.Fori(1, BATCH) as tb:
                down_low(tb, False)

        @block.tensor
        def _(pe):
            pe.wait_ge(silu_c_made, 1)
            for j in range(12):
                m, half = j // 2, j % 2
                pe.wait_ge(wmod_loaded[j % 3], 16 * (j // 3 + 1))
                wm = WM[j % 3]
                if m % 3 < 2:
                    for f in range(C):
                        for cc in range(C // 2):
                            last = pe.matmul(ps[:, MOD_BANK[m], f * BATCH:(f + 1) * BATCH],
                                             wm[:, cc, :].rearrange("k (p f) -> k f p", f=C)[:, f, :],
                                             SC[:, 4 * half + cc, :],
                                             start=(half == 0 and f == 0 and cc == 0), stop=(half == 1 and cc == 3),
                                             skip_group_check=True)
                else:
                    if m == 5 and half == 0:
                        pe.wait_ge(gate_step, 2)
                    for hb in range(2):
                        for cc in range(C // 2):
                            last = pe.matmul(ps[0:BATCH, 1 + hb, :], SC[:, 4 * half + cc, :],
                                             wm[:, cc, hb * HALF:(hb + 1) * HALF],
                                             start=(half == 0 and cc == 0), stop=(half == 1 and cc == 3))
                last.then_inc(wmod_used, 1)
                if j == 1:
                    pe.wait_ge(consts_made, 2)
                    pe.wait_ge(mask_step, 5)
                    pe.matmul(ps[:, MASK_BANK, 0:D // MASK_B], GROUP[:], MCOL[:], start=True, stop=True).then_inc(mask_summed, 1)

            def turn(u, par, src, fresh):
                if not fresh:
                    pe.wait_ge(modulated, u - 1)
                for c in range(C):
                    last = pe.transpose(ps[:, 4 + 2 * par + c // 4, (c % 4) * P:(c % 4 + 1) * P],
                                        src.rearrange("t (p c) -> t c p", c=C)[:, c, :], IDENT[:])
                last.then_inc(turned, 1)

            def attend(b, k):
                t = TPB * b + k
                par = k % 2
                pe.wait_ge(tile_lo, t + 1)
                if not (isinstance(t, int) and t < 2):
                    pe.wait_ge(gated, t - 1)
                for hb in range(2):
                    acc = ps[:, 2 * par + hb, :]
                    cols = slice(hb * HALF, (hb + 1) * HALF)
                    for c in range(C):
                        pe.matmul(acc, AH[par][:, c, :], WH[:, c, cols], start=(c == 0), stop=False)
                        pe.matmul(acc, AH[par][:, c, :], WL[:, c, cols], start=False, stop=False)
                        last = pe.matmul(acc, AL[par][:, c, :], WH[:, c, cols], start=False, stop=(c == C - 1))
                return last.then_inc(attn_done, 1)

            pe.wait_ge(w_lo, 4)
            pe.wait_ge(ln_step, LN_STEPS)
            turn(0, 0, XN[0][:], True)

            def attn_step(b, k, has_next):
                t = TPB * b + k
                if has_next:
                    first = isinstance(t, int) and t == 0
                    pe.wait_ge(ln_step, LN_STEPS * (ln_index(0, t + 1) + 1))
                    turn(t + 1, (k + 1) % 2, XN[(k + 1) % 2][:], first)
                attend(b, k)

            for k in range(TPB):
                attn_step(0, k, True)
            with pe.Fori(1, BATCH - 1) as b:
                for k in range(TPB):
                    attn_step(b, k, True)
            for k in range(TPB):
                attn_step(BATCH - 1, k, k < TPB - 1)
            pe.wait_ge(attn_done, TILES)
            pe.sem_inc(stage_done, 1)

            with pe.Fori(0, BATCH) as b:
                for k in range(TPB):
                    t = TPB * b + k
                    pe.wait_ge(xn2_loaded[k], 16 * (b + 1))
                    turn(TILES + t, k % 2, X[k][:], False)

            def up_block(c, cpar, b):
                banks = [2 * b, 2 * b + 1]
                pe.wait_ge(h_made, TPB * c + b + 1 if not isinstance(c, int) or c > 0 else TPB)
                for w in range(2):
                    ring = 2 * cpar + w
                    if b == 0:
                        pe.wait_ge(w12_lo, 2 * c + w + 1)
                    for k in range(C):
                        acc = ps[:, banks[w], :]
                        pe.matmul(acc, RH[ring][:, k, :], HH[:, b, k, :], start=(k == 0), stop=False)
                        pe.matmul(acc, RH[ring][:, k, :], HL[:, b, k, :], start=False, stop=False)
                        last = pe.matmul(acc, RL[ring][:, k, :], HH[:, b, k, :], start=False, stop=(k == C - 1))
                return last

            def up_step(c, cpar):
                for b in range(TPB):
                    up_block(c, cpar, b).then_inc(up_done, 1)
                pe.wait_ge(up_done, TPB * (c + 1))
                pe.sem_inc(stage_done, 1)

            up_step(0, 0)
            up_step(1, 1)
            with pe.Fori(1, PAIRS) as i:
                up_step(2 * i, 0)
                up_step(2 * i + 1, 1)
            for c in range(2 * PAIRS, FULL):
                up_step(c, c % 2)
            c, ring = FULL, 2 * (FULL % 2)
            pe.wait_ge(w12_lo, 2 * FULL + 1)
            for b in range(TPB):
                pe.wait_ge(h_made, TPB * c + b + 1)
                acc = ps[:, 2 * b, :]
                for k in range(C):
                    pe.matmul(acc, RH[ring][:, k, :], HH[:, b, k, :], start=(k == 0), stop=False)
                    pe.matmul(acc, RH[ring][:, k, :], HL[:, b, k, :], start=False, stop=False)
                    last = pe.matmul(acc, RL[ring][:, k, :], HH[:, b, k, :], start=False, stop=(k == C - 1))
                last.then_inc(up_done, 1)
            pe.wait_ge(up_done, TPB * CH)
            pe.sem_inc(stage_done, 1)

            def down_chunk(tb, ch, par, with_w3):
                rows = TAIL if isinstance(ch, int) and ch == CH - 1 else P
                first, final = isinstance(ch, int) and ch == 0, isinstance(ch, int) and ch == CH - 1
                g = tb * CH + ch
                pe.wait_ge(h_lo, g + 1)
                if with_w3:
                    pe.wait_ge(w3_lo, ch + 1)
                for k in range(TPB):
                    if first:
                        if isinstance(tb, int):
                            pe.wait_ge(h_made, TPB * (CH + 1))
                        else:
                            pe.wait_ge(y_gated, TPB * (tb - 1) + k + 1)
                    tok = slice(k * P, (k + 1) * P)
                    hi, lo = HHI[par][0:rows, tok], HLO[par][0:rows, tok]
                    for lhs, w in ((hi, W3H), (hi, W3L), (lo, W3H)):
                        for hb in range(2):
                            last = pe.matmul(ps[:, 2 * k + hb, :], lhs, w[0:rows, ch, hb * HALF:(hb + 1) * HALF],
                                             start=(first and lhs is hi and w is W3H), stop=(final and lhs is lo))
                last.then_inc(h_used, 1)

            def down(tb, with_w3):
                for ch in range(2):
                    down_chunk(tb, ch, ch, with_w3)
                with pe.Fori(1, CH // 2 - 1) as i:
                    for k in range(2):
                        down_chunk(tb, 2 * i + k, k, with_w3)
                for ch in range(CH - 2, CH):
                    down_chunk(tb, ch, ch % 2, with_w3)

            down(0, True)
            with pe.Fori(1, BATCH) as tb:
                down(tb, False)


def kernel(**inputs):
    import concourse.bacc as bacc
    from concourse.bass_utils import run_bass_kernel_spmd

    a = {k: np.asarray(v) for k, v in inputs.items()}
    w1, w2 = a["L0_ffn_w1_q"].T, a["L0_ffn_w2_q"].T
    s1, s2 = a["L0_ffn_w1_scale"].T, a["L0_ffn_w2_scale"].T

    def tiles(m, rows):
        full = m[:, :FULL * P].reshape(rows, -1, FULL, P)
        return full.transpose(2, 0, 1, 3)

    def pairs(m1, m2, rows):
        both = np.stack([tiles(m1, rows), tiles(m2, rows)], axis=1)
        both = both.reshape(2 * FULL, rows, -1, P)
        tail = np.concatenate([m1[:, FULL * P:].reshape(rows, -1, TAIL), m2[:, FULL * P:].reshape(rows, -1, TAIL)], axis=2)
        return np.ascontiguousarray(np.concatenate([both, tail[None]], axis=0).reshape(2 * FULL + 1, rows, -1))

    arrays = {
        "cT": np.ascontiguousarray(a["L0_c"].T).reshape(P, C * BATCH),
        "x": a["L0_attn_data"].reshape(TOK, D),
        "w12q": pairs(w1, w2, P),
        "w12s": pairs(s1, s2, D // NF4B),
        "w3q": np.ascontiguousarray(a["L0_ffn_w3_q"].T),
        "w3s": np.ascontiguousarray(a["L0_ffn_w3_scale"].T),
        "wT": np.ascontiguousarray(a["L0_attn_weight"].T),
        "maskT": np.ascontiguousarray(a["L0_attn_mask"].T),
        "wmod": a["L0_wmod"],
    }
    nc = bacc.Bacc("TRN2", target_bir_lowering=False, num_devices=1)
    args = [nc.dram_tensor(n, v.shape, mybir.dt.from_np(v.dtype), kind="ExternalInput").ap() for n, v in arrays.items()]
    out = nc.dram_tensor("out", (TOK, D), F32, kind="ExternalOutput").ap()
    adaln_kernel(nc, *args, out)
    r = run_bass_kernel_spmd(nc, [arrays], core_ids=[0])
    return r.results[0]["out"].reshape(BATCH, SEQ, D)
```

```python
import numpy as np
import concourse.bass as bass
from concourse import mybir

F32, F32R, I32 = mybir.dt.float32, mybir.dt.float32r, mybir.dt.int32
ALU, ACT, AXL = mybir.AluOpType, mybir.ActivationFunctionType, mybir.AxisListType

P = 128
BATCH, SEQ, D, HID = 4, 512, 1024, 2752
TOK = BATCH * SEQ
TILES = TOK // P
TPB = SEQ // P
C = D // P
NF4B = 64
FULL = HID // P
CH = FULL + 1
PAIRS = FULL // 2 - 1
LOWER = 18
TAIL = HID - FULL * P
HALF = 512
MASK_B = 32
EPS = 1e-5
KB = 1024

NF4 = [-1.0, -0.6961928009986877, -0.5250730514526367, -0.39491748809814453, -0.28444138169288635,
       -0.18477343022823334, -0.09105003625154495, 0.0, 0.07958029955625534, 0.16093020141124725,
       0.24611230194568634, 0.33791524171829224, 0.44070982933044434, 0.5626170039176941, 0.7229568362236023, 1.0]


def nf4_lines():
    table = np.array(NF4, np.float32).astype(np.float64)
    lines = []
    for q in range(0, 16, 2):
        best = None
        slope = np.float32(table[q + 1] - table[q])
        for da in range(-40, 41):
            a = np.float32(slope + da * np.spacing(slope))
            offset = np.float32(table[q] - np.float64(a) * q)
            for db in (-1, 0, 1):
                b = np.float32(offset + db * np.spacing(offset))
                got = [float(np.float32(np.float64(a) * k + np.float64(b))) for k in (q, q + 1)]
                off = [abs(got[0] - table[q]), abs(got[1] - table[q + 1])]
                if q == 6:
                    off[1] = 0.0 if got[1] >= 0 else 1.0
                key = (max(off), sum(off), abs(da))
                if best is None or key < best[0]:
                    best = (key, float(a), float(b))
        lines.append(best[1:])
    return lines


LINES = nf4_lines()
NL = len(LINES)
READ_BY = [0, 0, 1, 2, 3, 3, 4, 5]
LSLOTS = 3
CSTEPS = 8


def adaln_kernel(nc, cT, x, w12q, w12s, w3q, w3s, wT, maskT, wmod, out):
    base = (nc.sbuf_base + 31) // 32 * 32

    def at(name, shape, dt, kb):
        return nc.alloc_sbuf_tensor_at(name, [P] + shape, dt, offset=base + int(kb * KB))

    HH = at("ffn_in_hi", [BATCH, C, SEQ], F32R, 0)
    HL = at("ffn_in_lo", [BATCH, C, SEQ], F32R, 64)
    WH = at("attn_w_hi", [C, D], F32R, 32)
    WL = at("attn_w_lo", [C, D], F32R, 96)
    WM = [at(f"wmod_{i}", [C // 2, D], F32, kb) for i, kb in enumerate((0, 16, 64))]
    MP = [at(f"mask_piece_{i}", [2, D], I32, kb) for i, kb in enumerate((80, 88))]
    WP = [at(f"weight_piece_{i}", [2, D], F32, kb) for i, kb in enumerate((80, 88))]
    RH = [at(f"w12_hi_{i}", [C, P], F32R, 128 + 4 * i) for i in range(4)]
    RL = [at(f"w12_lo_{i}", [C, P], F32R, 144 + 4 * i) for i in range(4)]
    AH = [at(f"attn_in_hi_{i}", [C, P], F32R, 136 + 4 * i) for i in range(2)]
    AL = [at(f"attn_in_lo_{i}", [C, P], F32R, 152 + 4 * i) for i in range(2)]
    ST = 160
    Q = [at(f"codes_{i}", [C * P], I32, ST + 4 * i) for i in range(2)]
    ACC = [at(f"decoded_{i}", [C * P], F32, ST + 8 + 4 * i) for i in range(2)]
    POS = at("positive_part", [C * P], F32, ST + 16)
    L = [at(f"line_{i}", [C * P], F32, ST + 20 + 4 * i) for i in range(LSLOTS)]
    S12 = [at(f"w12_scale_{i}", [P], F32, ST + 32 + 0.5 * i) for i in range(2)]
    S3 = at("w3_scale", [D], F32, ST + 33)
    SG = at("silu_g", [HALF], F32, ST + 37)
    HT = [at(f"h_tile_{i}", [HALF], F32, ST + 39 + 2 * i) for i in range(2)]
    X = [at(f"x_{i}", [D], F32, ST + 4 * i) for i in range(4)]
    XN = [at(f"normed_{i}", [D], F32, ST + 16 + 4 * i) for i in range(2)]
    HM = [at(f"modulated_{i}", [C, P], F32, ST + 24 + 4 * i) for i in range(2)]
    GA = at("attn_gate", [D], F32, ST + 32)
    XN2 = [at(f"normed_again_{i}", [D], F32, ST + 36 + 4 * i) for i in range(2)]
    MSUM = at("mask_sums", [C, D // MASK_B], F32, ST + 40)
    MCOL, BMASK = (at(n, [D // MASK_B], F32, ST + kb) for n, kb in (("mask_column", 41), ("block_mask", 41.25)))
    W3H = at("w3_hi", [CH, D], F32R, 0)
    W3L = at("w3_lo", [LOWER, D], F32R, 88)
    W3LT = at("w3_lo_top", [CH - LOWER, D], F32R, 191.75)
    DN = 160
    HR = [at(f"h_raw_{i}", [HALF], F32, DN + 2 * i) for i in range(2)]
    HHI = [at(f"h_hi_{i}", [HALF], F32R, DN + 4 + 2 * i) for i in range(2)]
    HLO = [at(f"h_lo_{i}", [HALF], F32R, DN + 8 + 2 * i) for i in range(2)]
    GB = at("ffn_gate", [D], F32, DN + 12)
    YG = at("gated", [D], F32, DN + 16)
    X2 = [at(f"x2_{i}", [D], F32, DN + 20 + 4 * i) for i in range(2)]
    W3R = [at(f"w3_raw_{i}", [D], F32, DN + 20 + 4 * i) for i in range(2)]

    def w3_low_part(ch):
        return W3LT[:, ch - LOWER, :] if isinstance(ch, int) and ch >= LOWER else W3L[:, ch, :]

    free = [ST + 44]

    def small(name, shape, dt=F32):
        t = at(name, shape, dt, free[0])
        free[0] += (int(np.prod(shape)) * 4 + 31) // 32 * 32 / KB
        return t

    IDENT = small("identity", [P])
    GROUP = small("four_partition_groups", [P])
    CT, SC = small("c", [C, BATCH]), small("silu_c", [C, BATCH])
    MODS = [small(f"mod_{i}", [BATCH, 2 * C]) for i in range(2)]
    SGN, MAG = small("gate_sign", [BATCH * C]), small("gate", [BATCH * C])
    GT = small("gate_rows", [P])
    STATS = [[small(f"stats_{k}{i}", [12]) for i in range(2)] for k in range(2)]
    MV = [[small(f"mean_var_{k}{i}", [2]) for i in range(2)] for k in range(2)]
    VE = [[small(f"var_eps_{k}{i}", [1]) for i in range(2)] for k in range(2)]
    SD = [[small(f"std_{k}{i}", [1]) for i in range(2)] for k in range(2)]
    RS = [[small(f"rstd_{k}{i}", [1]) for i in range(2)] for k in range(2)]
    T1 = [[small(f"newton_{k}{i}", [1]) for i in range(2)] for k in range(2)]
    T2 = [[small(f"newton_factor_{k}{i}", [1]) for i in range(2)] for k in range(2)]
    NB = [small(f"neg_mean_rstd_{i}", [1]) for i in range(2)]
    RF = [[small(f"rstd_fine_{k}{i}", [1]) for i in range(2)] for k in range(2)]

    ps = nc.alloc_psum_tensor("ps", [P, 8, HALF], F32)

    gates_d = nc.dram_tensor("gates_d", (2, BATCH, D), F32, kind="Internal").ap()
    x2_d = nc.dram_tensor("x2_d", (TOK, D), F32, kind="Internal").ap()
    xn2_d = nc.dram_tensor("xn2_d", (TOK, D), F32, kind="Internal").ap()
    h_d = nc.dram_tensor("h_d", (CH * P, TOK), F32, kind="Internal").ap()
    w3_d = nc.dram_tensor("w3_d", (CH * P, D), F32, kind="Internal").ap()

    sem = nc.alloc_semaphore
    c_loaded, ga_loaded, gb_loaded = sem("c_loaded"), sem("ga_loaded"), sem("gb_loaded")
    gate_stored = sem("gate_stored")
    codes_loaded = [sem(f"codes_loaded_{i}") for i in range(2)]
    s12_loaded = [sem(f"s12_loaded_{i}") for i in range(2)]
    s3_loaded = sem("s3_loaded")
    wmod_loaded = [sem(f"wmod_loaded_{i}") for i in range(3)]
    piece_loaded = [sem(f"piece_loaded_{i}") for i in range(2)]
    x_loaded = [sem(f"x_loaded_{i}") for i in range(4)]
    x2_stored = [sem(f"x2_stored_{i}") for i in range(4)]
    xn2_stored = [sem(f"xn2_stored_{i}") for i in range(2)]
    xn2_loaded = [sem(f"xn2_loaded_{i}") for i in range(4)]
    h_stored = [sem(f"h_stored_{i}") for i in range(2)]
    w3_stored = sem("w3_stored")
    h_loaded = [sem(f"h_loaded_{i}") for i in range(2)]
    w3_loaded = [sem(f"w3_loaded_{i}") for i in range(2)]
    x2_loaded = [sem(f"x2_loaded_{i}") for i in range(2)]
    out_stored = [sem(f"out_stored_{i}") for i in range(2)]
    consts_made = sem("consts_made")
    pool_step = sem("pool_step")
    silu_c_made = sem("silu_c_made")
    wmod_used = sem("wmod_used")
    mod_read = sem("mod_read")
    gate_step = sem("gate_step")
    mask_step = sem("mask_step")
    mask_summed = sem("mask_summed")
    piece_masked = sem("piece_masked")
    w_hi = sem("w_hi")
    w_lo = sem("w_lo")
    line_ready = sem("line_ready")
    combined = sem("combined")
    w12_hi = sem("w12_hi")
    w12_lo = sem("w12_lo")
    ln1_step, ln2_step = sem("ln1_step"), sem("ln2_step")
    root1_done, root2_done = sem("root1_done"), sem("root2_done")
    normed1 = sem("normed1")
    turned1, turned2 = sem("turned1"), sem("turned2")
    modulated1, modulated2 = sem("modulated1"), sem("modulated2")
    high1, high2 = sem("high1"), sem("high2")
    low1, low2 = sem("low1"), sem("low2")
    gate_turned, gate_out = sem("gate_turned"), sem("gate_out")
    attn_done = sem("attn_done")
    gated = sem("gated")
    x2_made = sem("x2_made")
    stage_done = sem("stage_done")
    up_done = sem("up_done")
    silu_done = sem("silu_done")
    h_made = sem("h_made")
    h_hi, h_lo = sem("h_hi"), sem("h_lo")
    w3_hi, w3_lo = sem("w3_hi"), sem("w3_lo")
    block_done = sem("block_done")
    h_used = sem("h_used")
    y_gated = sem("y_gated")
    out_made = sem("out_made")

    MOD_BANK, MASK_BANK, GATE_BANK = (0, 1, 6, 6, 7, 6), 2, 7
    LN_STEPS, GATE_STEPS = 9, 5
    HALF_TILES = TILES // 2

    def batch_of(t):
        return (t // TPB + BATCH // 2) % BATCH

    def rows_of(t):
        r = batch_of(t) * SEQ + (t % TPB) * P
        return slice(r, r + P)

    def first_n(c):
        return 2 + 3 * c

    def tiles_of(c):
        if isinstance(c, int) and c == FULL:
            return [2]
        if isinstance(c, int) and c == FULL - 1:
            return [0, 2]
        return [0, 1, 2]

    def number(c, kind):
        if isinstance(c, int) and c == FULL:
            return first_n(FULL - 1) + 2
        if isinstance(c, int) and c == FULL - 1 and kind == 2:
            return first_n(c) + 1
        return first_n(c) + kind

    block = nc.Block()
    with block:

        @block.sync
        def _(sp):
            sp.dma_start(CT[:], cT.rearrange("p (c b) -> p c b", b=BATCH)).then_inc(c_loaded, 16)
            wmod_v = wmod.rearrange("(p c) f -> p c f", c=C)

            def load_wmod(j):
                if j >= 3:
                    sp.wait_ge(wmod_used, j - 2)
                m, half = j // 2, j % 2
                sp.dma_start(WM[j % 3][:], wmod_v[:, 4 * half:4 * half + 4, m * D:(m + 1) * D]).then_inc(wmod_loaded[j % 3], 16)

            def load_codes(n, src, slot):
                sp.dma_start(Q[slot][0:src.shape[0], :], src).then_inc(codes_loaded[slot], 16)

            def load_s12(tile, w):
                src = w12s[tile].unsqueeze(1).broadcast_to([P // 8, 8, P])
                sp.dma_start(S12[w][:], src).then_inc(s12_loaded[w], 16)

            for w in range(2):
                load_codes(w, w12q[w], w)
                load_s12(w, w)
                load_wmod(w)
            for j in range(2, 4):
                load_wmod(j)
            for t in range(4):
                sp.wait_ge(w12_lo, 2)
                sp.dma_start(X[t][:], x[rows_of(t), :]).then_inc(x_loaded[t], 16)
            for j in range(4, 9):
                load_wmod(j)

            def store_gate(g):
                sp.wait_ge(gate_out, g + 1)
                sp.dma_start(gates_d[g].rearrange("b (f p) -> (b f) p", p=P), GT[0:BATCH * C, :]).then_inc(gate_stored, 16)

            def load_ga(b):
                sp.dma_start(GA[:], gates_d[0, b].partition_broadcast(P)).then_inc(ga_loaded, 16)

            store_gate(0)
            sp.wait_ge(gate_stored, 16)
            load_ga(batch_of(0))

            for t in range(TILES):
                k = t % TPB
                sp.wait_ge(x2_made, t + 1)
                sp.dma_start(x2_d[rows_of(t), :], X[k][:]).then_inc(x2_stored[k], 16)
                if k == TPB - 1 and t < TILES - 1:
                    load_ga(batch_of(t + 1))
                sp.wait_ge(ln2_step, LN_STEPS * (t + 1))
                if t < HALF_TILES:
                    sp.dma_start(xn2_d[rows_of(t), :], XN2[t % 2][:]).then_inc(xn2_stored[t % 2], 16)
                if t + TPB < TILES:
                    sp.wait_ge(x2_stored[k], 16 * (t // TPB + 1))
                    sp.dma_start(X[k][:], x[rows_of(t + TPB), :]).then_inc(x_loaded[k], 16)
                if t < 3:
                    load_wmod(9 + t)
                if t == HALF_TILES:
                    store_gate(1)
                    sp.wait_ge(gate_stored, 32)

            for d in range(HALF_TILES):
                k = d % TPB
                if d < TPB:
                    sp.wait_ge(x2_stored[k], 16 * TILES // TPB)
                    if d < 2:
                        sp.wait_ge(xn2_stored[d], 16 * HALF_TILES // 2)
                else:
                    sp.wait_ge(turned2, HALF_TILES + d - TPB + 1)
                sp.dma_start(X[k][:], xn2_d[rows_of(d), :]).then_inc(xn2_loaded[k], 16)

            def fetch(n, c, kind):
                slot = (n if isinstance(n, int) else n_par[kind]) % 2
                if kind == 2:
                    rows = TAIL if isinstance(c, int) and c == CH - 1 else P
                    load_codes(n, w3q[bass.ds(c * P, rows), :], slot)
                    for g in range(rows // NF4B):
                        sp.dma_start(S3[g * NF4B:(g + 1) * NF4B, :],
                                     w3s[2 * c + g].partition_broadcast(NF4B)).then_inc(s3_loaded, 16)
                else:
                    load_codes(n, w12q[2 * c + 2 + kind], slot)
                    load_s12(2 * c + 2 + kind, kind)

            n_par = [0, 0, 0]

            def fetch_after(c, kind, par):
                n = number(c, kind)
                n_par[kind] = par
                if kind == 2 and isinstance(c, int) and c >= FULL - 1:
                    sp.wait_ge(combined, CSTEPS * (number(c - 1, 2) + 1))
                else:
                    sp.wait_ge(combined, CSTEPS * (n - 2))
                sp.wait_ge(line_ready, NL * (n - 1))
                fetch(n, c, kind)

            def store_h(c, b):
                sp.wait_ge(h_made, TPB * (c + 1) + b + 1)
                rows = TAIL if isinstance(c, int) and c == FULL else P
                sp.dma_start(h_d[bass.ds(c * P, rows), b * HALF:(b + 1) * HALF],
                             HT[b % 2][0:rows, :]).then_inc(h_stored[b % 2], 16)

            def store_w3(c, par):
                n = number(c, 2)
                sp.wait_ge(combined, CSTEPS * (n + 1))
                rows = TAIL if isinstance(c, int) and c == FULL else P
                sp.dma_start(w3_d[bass.ds(c * P, rows), :], ACC[par][0:rows, :]).then_inc(w3_stored, 16)

            def load_h(tb, ch, par):
                rows = TAIL if isinstance(ch, int) and ch == CH - 1 else P
                g = tb * CH + ch
                if not (isinstance(tb, int) and tb == 0 and isinstance(ch, int) and ch < 2):
                    sp.wait_ge(h_lo, g - 1)
                sp.dma_start(HR[par][0:rows, :], h_d[bass.ds(ch * P, rows), bass.ds(tb * HALF, HALF)])\
                  .then_inc(h_loaded[par], 16)

            def load_w3(ch, par):
                rows = TAIL if isinstance(ch, int) and ch == CH - 1 else P
                if not (isinstance(ch, int) and ch < 2):
                    sp.wait_ge(w3_lo, ch - 1)
                sp.dma_start(W3R[par][0:rows, :], w3_d[bass.ds(ch * P, rows), :]).then_inc(w3_loaded[par], 16)

            def up_io(c, cpar):
                seq = tiles_of(c)
                par = {kind: (cpar + i) % 2 for i, kind in enumerate(seq)}
                if seq == [2]:
                    par = {2: (first_n(FULL - 1) + 2) % 2}
                nxt = c + 1
                last = isinstance(c, int) and c == FULL
                nseq = [] if last else tiles_of(nxt)
                if seq[-1] == 2 and len(seq) == 3:
                    fetch_after(c, 2, par[2])
                if last:
                    store_w3(c, par[2])
                store_h(c, 0)
                if last:
                    sp.wait_ge(w3_stored, 16 * CH)
                    sp.wait_ge(line_ready, NL * (number(FULL, 2) + 1))
                    sp.wait_ge(h_stored[0], 16 * (FULL * TPB // 2 + 1))
                    sp.wait_ge(h_stored[1], 16 * (FULL * TPB // 2))
                    for ch in range(2):
                        load_h(0, ch, ch)
                        load_w3(ch, ch)
                npar = {kind: (cpar + 1 + i) % 2 for i, kind in enumerate(nseq)}
                if nseq == [2]:
                    npar = {2: (first_n(FULL - 1) + 2) % 2}
                if nseq:
                    fetch_after(nxt, nseq[0], npar[nseq[0]])
                store_h(c, 1)
                if len(nseq) > 1:
                    fetch_after(nxt, nseq[1], npar[nseq[1]])
                if not last:
                    store_w3(c, par[2])
                store_h(c, 2)
                store_h(c, 3)

            sp.wait_ge(turned2, TILES - 2)
            sp.wait_ge(gated, TILES)
            for kind in range(2):
                n_par[kind] = kind
                fetch(first_n(0) + kind, 0, kind)
            up_io(0, 0)
            up_io(1, 1)
            with sp.Fori(1, PAIRS) as i:
                up_io(2 * i, 0)
                up_io(2 * i + 1, 1)
            for c in range(2 * PAIRS, FULL):
                up_io(c, c % 2)
            up_io(FULL, FULL % 2)

            sp.wait_ge(stage_done, 1 + CH)
            for s in range(2):
                sp.wait_ge(h_stored[s], 16 * CH * TPB // 2)
            sp.wait_ge(w3_stored, 16 * CH)

            def store_out(tb, k):
                t = tb * TPB + k
                sp.wait_ge(out_made, t + 1)
                sp.dma_start(out[bass.ds(t * P, P), :], X2[k % 2][:]).then_inc(out_stored[k % 2], 16)

            def load_x2(tb, k):
                if k >= 2 or not (isinstance(tb, int) and tb == 0):
                    sp.wait_ge(out_stored[k % 2], 16 * (tb * (TPB // 2) + k // 2))
                sp.dma_start(X2[k % 2][:], x2_d[bass.ds((tb * TPB + k) * P, P), :]).then_inc(x2_loaded[k % 2], 16)

            def down_io(tb, more):
                first = isinstance(tb, int) and tb == 0
                if not first:
                    sp.wait_ge(y_gated, tb * TPB)
                sp.dma_start(GB[:], gates_d[1, tb].partition_broadcast(P)).then_inc(gb_loaded, 16)
                if not first:
                    for k in range(2):
                        load_x2(tb, k)
                with sp.Fori(1 if first else 2, CH // 2 - 1) as i:
                    for k in range(2):
                        load_h(tb, 2 * i + k, k)
                        if first:
                            load_w3(2 * i + k, k)
                for ch in range(CH - 2, CH):
                    load_h(tb, ch, ch % 2)
                    if first:
                        load_w3(ch, ch % 2)
                if first:
                    for k in range(2):
                        sp.wait_ge(w3_lo, CH - 1 + k)
                        load_x2(tb, k)
                if more:
                    load_h(tb + 1, 0, 0)
                    load_h(tb + 1, 1, 1)
                store_out(tb, 0)
                load_x2(tb, 2)
                store_out(tb, 1)
                load_x2(tb, 3)
                store_out(tb, 2)
                if more:
                    load_h(tb + 1, 2, 0)
                store_out(tb, 3)
                if more:
                    load_h(tb + 1, 3, 1)

            down_io(0, True)
            with sp.Fori(1, BATCH - 1) as tb:
                down_io(tb, True)
            down_io(BATCH - 1, False)
            for s in range(2):
                sp.wait_ge(out_stored[s], 16 * TILES // 2)

        @block.gpsimd
        def _(pool):
            pool.memset(IDENT[:], 0.0).then_inc(pool_step, 1)
            pool.memset(GROUP[:], 1.0).then_inc(pool_step, 1)
            pool.wait_ge(pool_step, 2)
            pool.affine_select(out=IDENT[:], in_=IDENT[:], compare_op=ALU.not_equal, fill=1.0, base=0,
                               pattern=[[-1, P]], channel_multiplier=1).then_inc(consts_made, 1)
            g3 = GROUP[:].rearrange("p (g o) -> p g o", o=4)
            pool.affine_select(out=g3, in_=g3, compare_op=ALU.is_ge, fill=0.0, base=0,
                               pattern=[[-4, P // 4], [0, 4]], channel_multiplier=1).then_inc(pool_step, 1)
            pool.wait_ge(pool_step, 3)
            pool.affine_select(out=g3, in_=g3, compare_op=ALU.is_ge, fill=0.0, base=3,
                               pattern=[[4, P // 4], [0, 4]], channel_multiplier=-1).then_inc(consts_made, 1)
            mask_v = maskT.rearrange("(p c) n -> p c n", c=C)
            w_v = wT.rearrange("(p c) n -> p c n", c=C)
            for j in range(8):
                if j >= 2:
                    if j - 2 < 4:
                        pool.wait_ge(mask_step, j - 1)
                    else:
                        pool.wait_ge(w_lo, j - 5)
                if j < 4:
                    pool.dma_start(MP[j % 2][:], mask_v[:, 2 * j:2 * j + 2, :]).then_inc(piece_loaded[j % 2], 16)
                else:
                    i = j - 4
                    pool.dma_start(WP[j % 2][:], w_v[:, 2 * i:2 * i + 2, :]).then_inc(piece_loaded[j % 2], 16)

        def line_free(eng, n, j):
            if j >= LSLOTS:
                eng.wait_ge(combined, CSTEPS * n + READ_BY[j - LSLOTS] + 1)
            elif not (isinstance(n, int) and n == 0):
                eng.wait_ge(combined, CSTEPS * (n - 1) + READ_BY[j - LSLOTS + NL] + 1)

        @block.scalar
        def _(act):
            act.wait_ge(c_loaded, 16)
            act.activation(SC[:], CT[:], ACT.Silu).then_inc(silu_c_made, 1)

            def lines(n, npar, first_line, codes_wait, rows=P):
                act.wait_ge(codes_loaded[npar], codes_wait)
                for j, (slope, offset) in enumerate(LINES):
                    line_free(act, n, j)
                    act.activation(L[(first_line + j) % LSLOTS][0:rows, :], Q[npar][0:rows, :], ACT.Copy,
                                   bias=offset, scale=slope).then_inc(line_ready, 1)

            def w12_high(n, npar, ring):
                act.wait_ge(combined, CSTEPS * (n + 1))
                act.activation(RH[ring][:], ACC[npar][:].rearrange("p (c h) -> p c h", c=C), ACT.Copy).then_inc(w12_hi, 1)

            for n in range(2):
                lines(n, n, NL * n, 16)
            for n in range(2):
                w12_high(n, n, n)
            for t in range(2):
                act.wait_ge(ln1_step, LN_STEPS * t + 4)
                act.activation(SD[0][t][:], VE[0][t][:], ACT.Sqrt).then_inc(root1_done, 1)
                act.wait_ge(ln1_step, LN_STEPS * (t + 1))
                act.activation(XN[t][:], X[t][:], ACT.Identity, bias=NB[t][:], scale=RF[0][t][:]).then_inc(normed1, 1)
            for j in range(4):
                act.wait_ge(piece_masked, j + 1)
                act.activation(WH[:, 2 * j:2 * j + 2, :], WP[j % 2][:], ACT.Copy).then_inc(w_hi, 1)

            def root(kind, t):
                step, done = ((ln1_step, root1_done), (ln2_step, root2_done))[kind]
                act.wait_ge(step, LN_STEPS * t + 4)
                act.activation(SD[kind][t % 2][:], VE[kind][t % 2][:], ACT.Sqrt).then_inc(done, 1)

            def norm1(t):
                act.wait_ge(ln1_step, LN_STEPS * (t + 1))
                if t >= 2:
                    act.wait_ge(turned1, t - 1)
                act.activation(XN[t % 2][:], X[t % TPB][:], ACT.Identity, bias=NB[t % 2][:],
                               scale=RF[0][t % 2][:]).then_inc(normed1, 1)

            def modulate(src, dst, mods, b, done, count):
                for c in range(C):
                    ins = act.activation(dst[:, c, :], ps[:, src + c // 4, (c % 4) * P:(c % 4 + 1) * P],
                                         ACT.Identity, bias=mods[:, b, c:c + 1], scale=mods[:, b, C + c:C + c + 1])
                ins.then_inc(done, 1)
                act.wait_ge(done, count)

            def input1(t):
                act.wait_ge(turned1, t + 1)
                if t >= 1:
                    act.wait_ge(low1, t)
                modulate(4, HM[0], MODS[0], batch_of(t), modulated1, t + 1)
                if t >= 2:
                    act.wait_ge(attn_done, t - 1)
                act.activation(AH[t % 2][:], HM[0][:], ACT.Copy).then_inc(high1, 1)

            def input2(e):
                s = 1 if e < HALF_TILES else e % 2
                act.wait_ge(turned2, e + 1)
                if e == HALF_TILES:
                    act.wait_ge(low1, TILES)
                    act.wait_ge(attn_done, TILES)
                elif e >= 1:
                    act.wait_ge(low2, e if e <= HALF_TILES + 1 else e - 1)
                if e == HALF_TILES + 1:
                    act.wait_ge(low2, HALF_TILES)
                modulate(4 + 2 * s, HM[s], MODS[1], e // TPB, modulated2, e + 1)
                b, k = e // TPB, e % TPB
                act.activation(HH[:, b, :, k * P:(k + 1) * P], HM[s][:], ACT.Copy).then_inc(high2, 1)

            def start1(t):
                root(0, t)
                norm1(t)

            act.wait_ge(mod_read, 2)
            input1(0)
            for t in range(TILES):
                if t == 1:
                    input1(2)
                    root(1, 0)
                else:
                    if t - 2 >= HALF_TILES:
                        input2(t - 2 - HALF_TILES)
                    if t >= 1:
                        root(1, t - 1)
                    if t + 1 < TILES:
                        input1(t + 1)
                if t + 2 < TILES:
                    start1(t + 2)
                if t == 5:
                    act.wait_ge(mod_read, 4)
            input2(HALF_TILES - 2)
            root(1, TILES - 1)
            for e in range(HALF_TILES - 1, TILES):
                input2(e)
            act.wait_ge(low2, TILES)

            def silu(c, b, rows=P):
                if b < TPB - 1:
                    act.wait_ge(up_done, (TPB - 1) * c + b + 1)
                else:
                    act.wait_ge(stage_done, c + 2)
                if not (isinstance(c, int) and c == 0 and b == 0):
                    act.wait_ge(h_made, TPB * (c + 1) + b)
                act.activation(SG[0:rows, :], ps[0:rows, 2 * b, :], ACT.Silu).then_inc(silu_done, 1)

            def up_step(c, cpar):
                seq = tiles_of(c)
                for i, kind in enumerate(seq):
                    n = number(c, kind)
                    npar = (cpar + i) % 2 if len(seq) > 1 else n % 2
                    rows = TAIL if seq == [2] else P
                    first = NL * number(c if isinstance(c, int) else cpar, kind)
                    lines(n, npar, first, codes_wait_value(n, npar), rows)
                    if i > 0 and seq[i - 1] != 2:
                        prev = seq[i - 1]
                        act.wait_ge(stage_done, c + 1)
                        w12_high(n - 1, (npar + 1) % 2, 2 * ((cpar + 1) % 2) + prev)
                    silu(c, i)
                for b in range(len(seq), TPB):
                    silu(c, b, TAIL if seq == [2] else P)

            def codes_wait_value(n, npar):
                return 16 * (n // 2 + 1) if isinstance(n, int) else 8 * (n - npar) + 16

            up_step(0, 0)
            up_step(1, 1)
            with act.Fori(1, PAIRS) as i:
                up_step(2 * i, 0)
                up_step(2 * i + 1, 1)
            for c in range(2 * PAIRS, FULL):
                up_step(c, c % 2)
            c = FULL
            n = number(c, 2)
            lines(n, n % 2, NL * n, codes_wait_value(n, n % 2), TAIL)

            def high(tb, ch, par, with_w3):
                rows = TAIL if isinstance(ch, int) and ch == CH - 1 else P
                g = tb * CH + ch
                count = 16 * (tb * (CH // 2) + ch // 2 + 1) if isinstance(ch, int) else 16 * (tb * (CH // 2)) + 8 * (ch - par) + 16
                act.wait_ge(h_loaded[par], count)
                if not (isinstance(g, int) and g < 2):
                    act.wait_ge(h_used, g - 1)
                act.activation(HHI[par][0:rows, :], HR[par][0:rows, :], ACT.Copy).then_inc(h_hi, 1)
                if with_w3:
                    act.wait_ge(w3_loaded[par], count)
                    act.activation(W3H[0:rows, ch, :], W3R[par][0:rows, :], ACT.Copy).then_inc(w3_hi, 1)

            def down_high(tb, with_w3):
                if not with_w3:
                    for ch in range(2):
                        high(tb, ch, ch, with_w3)
                with act.Fori(1, CH // 2 - 1) as i:
                    for k in range(2):
                        high(tb, 2 * i + k, k, with_w3)
                for ch in range(CH - 2, CH):
                    high(tb, ch, ch % 2, with_w3)

            silu(c, 0, TAIL)
            silu(c, 1, TAIL)
            act.wait_ge(line_ready, NL * (n + 1))
            act.wait_ge(up_done, (TPB - 1) * FULL + 1)
            high(0, 0, 0, True)
            silu(c, 2, TAIL)
            high(0, 1, 1, True)
            silu(c, 3, TAIL)
            act.wait_ge(stage_done, 1 + CH)
            down_high(0, True)
            with act.Fori(1, BATCH) as tb:
                down_high(tb, False)

        @block.vector
        def _(dve):
            def combine(n, npar, first_line, scale, scale_sem, scale_count, rows=P):
                acc, pos = ACC[npar][0:rows, :], POS[0:rows, :]

                def line(j):
                    return L[(first_line + j) % LSLOTS][0:rows, :]

                def step(k, j):
                    dve.wait_ge(line_ready, NL * n + j + 1)
                    if not (isinstance(n, int) and n == 0 and k == 0):
                        dve.wait_ge(combined, CSTEPS * n + k)

                step(0, 1)
                dve.tensor_tensor(acc, line(0), line(1), ALU.min).then_inc(combined, 1)
                step(1, 2)
                dve.scalar_tensor_tensor(out=acc, in0=line(2), scalar=0.0, in1=acc, op0=ALU.min, op1=ALU.min).then_inc(combined, 1)
                step(2, 3)
                dve.tensor_tensor(acc, line(3), acc, ALU.min).then_inc(combined, 1)
                step(3, 5)
                dve.scalar_tensor_tensor(out=pos, in0=line(4), scalar=0.0, in1=line(5), op0=ALU.max, op1=ALU.max).then_inc(combined, 1)
                step(4, 6)
                dve.tensor_tensor(pos, line(6), pos, ALU.max).then_inc(combined, 1)
                step(5, 7)
                dve.tensor_tensor(pos, line(7), pos, ALU.max).then_inc(combined, 1)
                step(6, 7)
                dve.tensor_tensor(acc, acc, pos, ALU.add).then_inc(combined, 1)
                step(7, 7)
                dve.wait_ge(scale_sem, scale_count)
                if scale.shape[1] == P:
                    acc3 = acc.rearrange("p (c h) -> p c h", c=C)
                    dve.tensor_tensor(acc3, acc3, scale.unsqueeze(1).broadcast_to([P, C, P]), ALU.mult).then_inc(combined, 1)
                else:
                    dve.tensor_tensor(acc, acc, scale, ALU.mult).then_inc(combined, 1)

            def w12_low(n, npar, ring, count):
                dve.wait_ge(w12_hi, count)
                dve.wait_ge(combined, CSTEPS * (n + 1))
                dve.tensor_tensor(RL[ring][:], ACC[npar][:].rearrange("p (c h) -> p c h", c=C),
                                  RH[ring][:].bitcast(F32), ALU.subtract).then_inc(w12_lo, 1)

            for n in range(2):
                combine(n, n, NL * n, S12[n][:], s12_loaded[n], 16)
            for n in range(2):
                w12_low(n, n, n, n + 1)

            def read_mod(m):
                dve.wait_ge(wmod_used, 2 * (m + 1))
                ln, s = m // 3, m % 3
                src = ps[:, MOD_BANK[m], 0:C * BATCH].rearrange("p (c b) -> p b c", b=BATCH)
                dve.tensor_scalar(MODS[ln][:, :, s * C:(s + 1) * C], src, float(s), None, ALU.add).then_inc(mod_read, 1)

            def gate(g):
                dve.wait_ge(wmod_used, 6 * (g + 1))
                src = ps[:, MOD_BANK[3 * g + 2], 0:C * BATCH].rearrange("p (c b) -> p b c", b=BATCH)
                sgn, mag = SGN[:], MAG[:]
                if g:
                    dve.wait_ge(gate_turned, g)
                dve.tensor_scalar(sgn.rearrange("p (b c) -> p b c", b=BATCH), src, 0.0, 2.0, ALU.is_ge, ALU.mult).then_inc(gate_step, 1)
                dve.tensor_copy(mag.rearrange("p (b c) -> p b c", b=BATCH), src).then_inc(gate_step, 1)
                dve.wait_ge(gate_step, GATE_STEPS * g + 2)
                dve.scalar_tensor_tensor(out=mag, in0=mag, scalar=-1.0, in1=mag, op0=ALU.mult, op1=ALU.max).then_inc(gate_step, 1)
                dve.wait_ge(gate_step, GATE_STEPS * g + 3)
                dve.tensor_scalar(mag, mag, 0.25, None, ALU.max).then_inc(gate_step, 1)
                dve.wait_ge(gate_step, GATE_STEPS * g + 4)
                dve.scalar_tensor_tensor(out=mag, in0=sgn, scalar=-1.0, in1=mag, op0=ALU.add, op1=ALU.mult).then_inc(gate_step, 1)

            def gate_rows(g):
                dve.wait_ge(gate_turned, g + 1)
                if g:
                    dve.wait_ge(gate_stored, 16 * g)
                dve.tensor_copy(GT[0:BATCH * C, :], ps[0:BATCH * C, GATE_BANK, 0:P]).then_inc(gate_out, 1)

            def statistics(kind, t, src):
                k, i = t % 2, LN_STEPS * t
                step, done = ((ln1_step, root1_done), (ln2_step, root2_done))[kind]
                st, mv, ve, sd = STATS[kind][k], MV[kind][k], VE[kind][k], SD[kind][k]
                rs, t1, t2, rf = RS[kind][k], T1[kind][k], T2[kind][k], RF[kind][k]
                dve.bn_stats(st[:, 0:6], src[:, 0:HALF]).then_inc(step, 1)
                dve.bn_stats(st[:, 6:12], src[:, HALF:D]).then_inc(step, 1)
                dve.wait_ge(step, i + 2)
                dve.memset(ve[:], EPS)
                dve.bn_aggr(mv[:], st[:]).then_inc(step, 1)
                dve.wait_ge(step, i + 3)
                dve.tensor_tensor(ve[:], mv[:, 1:2], ve[:], ALU.add).then_inc(step, 1)
                dve.wait_ge(done, t + 1)
                dve.reciprocal(rs[:], sd[:]).then_inc(step, 1)
                dve.wait_ge(step, i + 5)
                dve.scalar_tensor_tensor(out=t1[:], in0=rs[:], scalar=ve[:], in1=rs[:], op0=ALU.mult, op1=ALU.mult).then_inc(step, 1)
                dve.wait_ge(step, i + 6)
                dve.tensor_scalar(t2[:], t1[:], -0.5, 1.5, ALU.mult, ALU.add).then_inc(step, 1)
                dve.wait_ge(step, i + 7)
                if kind == 0 and t >= 2:
                    dve.wait_ge(normed1, t - 1)
                dve.tensor_tensor(rf[:], rs[:], t2[:], ALU.mult).then_inc(step, 1)
                dve.wait_ge(step, i + 8)

            def ln1(t):
                k = t % 2
                dve.wait_ge(x_loaded[t % TPB], 16 * (t // TPB + 1))
                statistics(0, t, X[t % TPB][:])
                dve.scalar_tensor_tensor(out=NB[k][:], in0=MV[0][k][:, 0:1], scalar=-1.0, in1=RF[0][k][:],
                                         op0=ALU.mult, op1=ALU.mult).then_inc(ln1_step, 1)

            def low_part1(t):
                dve.wait_ge(high1, t + 1)
                dve.tensor_tensor(AL[t % 2][:], HM[0][:], AH[t % 2][:].bitcast(F32), ALU.subtract).then_inc(low1, 1)

            def low_part2(e):
                s = 1 if e < HALF_TILES else e % 2
                b, k = e // TPB, e % TPB
                dve.wait_ge(high2, e + 1)
                dve.tensor_tensor(HL[:, b, :, k * P:(k + 1) * P], HM[s][:],
                                  HH[:, b, :, k * P:(k + 1) * P].bitcast(F32), ALU.subtract).then_inc(low2, 1)

            def residual(t):
                k, two = t % TPB, XN2[t % 2][:]
                dve.wait_ge(attn_done, t + 1)
                if k == 0:
                    dve.wait_ge(ga_loaded, 16 * (t // TPB + 1))
                if 2 <= t < HALF_TILES + 2:
                    dve.wait_ge(xn2_stored[t % 2], 16 * (t // 2))
                elif t >= 2:
                    dve.wait_ge(turned2, t - 1 - HALF_TILES)
                attn = ps[:, 2 * (t % 2):2 * (t % 2) + 2, :].rearrange("p a n -> p (a n)")
                dve.tensor_tensor(two, attn, GA[:], ALU.mult).then_inc(gated, 1)
                dve.wait_ge(gated, t + 1)
                dve.wait_ge(normed1, t + 1)
                dve.tensor_tensor(X[k][:], X[k][:], two, ALU.add).then_inc(x2_made, 1)
                dve.wait_ge(x2_made, t + 1)
                statistics(1, t, X[k][:])
                dve.tensor_scalar(two, X[k][:], MV[1][t % 2][:, 0:1], RF[1][t % 2][:], ALU.subtract, ALU.mult).then_inc(ln2_step, 1)

            for j in range(4):
                dve.wait_ge(piece_loaded[j % 2], 16 * (j // 2 + 1))
                dve.tensor_reduce(MSUM[:, 2 * j:2 * j + 2, :], MP[j % 2][:].rearrange("p c (n o) -> p c n o", o=MASK_B),
                                  AXL.X, ALU.add).then_inc(mask_step, 1)
            dve.wait_ge(mask_step, 4)
            dve.tensor_reduce(MCOL[:], MSUM[:].rearrange("p c n -> p n c"), AXL.X, ALU.add).then_inc(mask_step, 1)
            dve.wait_ge(mask_summed, 1)
            dve.tensor_scalar(BMASK[:], ps[:, MASK_BANK, 0:D // MASK_B], 0.0, None, ALU.is_gt).then_inc(mask_step, 1)
            dve.wait_ge(mask_step, 6)
            ln1(0)
            ln1(1)
            for m in range(2):
                read_mod(m)
            for j in range(4):
                dve.wait_ge(piece_loaded[j % 2], 16 * (j // 2 + 3))
                w4 = WP[j % 2][:].rearrange("p c (n o) -> p c n o", o=MASK_B)
                dve.tensor_tensor(w4, w4, BMASK[:].unsqueeze(1).unsqueeze(3).broadcast_to([P, 2, D // MASK_B, MASK_B]),
                                  ALU.mult).then_inc(piece_masked, 1)
                dve.wait_ge(w_hi, j + 1)
                dve.tensor_tensor(WL[:, 2 * j:2 * j + 2, :], WP[j % 2][:], WH[:, 2 * j:2 * j + 2, :].bitcast(F32),
                                  ALU.subtract).then_inc(w_lo, 1)

            low_part1(0)
            for t in range(TILES):
                if t == 1:
                    low_part1(2)
                    gate(0)
                    gate_rows(0)
                    residual(0)
                else:
                    if t >= 1:
                        residual(t - 1)
                    if t - 2 >= HALF_TILES:
                        low_part2(t - 2 - HALF_TILES)
                    if t + 1 < TILES:
                        low_part1(t + 1)
                if t + 2 < TILES:
                    ln1(t + 2)
                if t in (3, 5):
                    read_mod(3 if t == 3 else 4)
                if t == 7:
                    gate(1)
                if t == 8:
                    gate_rows(1)
            residual(TILES - 1)
            for e in range(HALF_TILES - 2, TILES):
                low_part2(e)
            dve.wait_ge(turned2, TILES)
            dve.sem_inc(h_made, TPB)

            def make_h(c, b):
                dve.wait_ge(silu_done, TPB * c + b + 1)
                if isinstance(c, int) and c == 0 and b < 2:
                    pass
                else:
                    dve.wait_ge(h_stored[b % 2], 16 * ((TPB // 2) * c + b // 2))
                if isinstance(c, int) and c == FULL:
                    dve.tensor_tensor(HT[b % 2][0:TAIL, :], SG[0:TAIL, :], ps[TAIL:2 * TAIL, 2 * b, :], ALU.mult).then_inc(h_made, 1)
                else:
                    dve.tensor_tensor(HT[b % 2][:], SG[:], ps[:, 2 * b + 1, :], ALU.mult).then_inc(h_made, 1)

            def up_step(c, cpar):
                seq = tiles_of(c)
                for i, kind in enumerate(seq):
                    n = number(c, kind)
                    npar = (cpar + i) % 2 if len(seq) > 1 else n % 2
                    rows = TAIL if seq == [2] else P
                    first = NL * number(c if isinstance(c, int) else cpar, kind)
                    if kind == 1 and not (isinstance(c, int) and c == 0):
                        dve.wait_ge(w3_stored, 16 * c)
                    if kind == 2 and isinstance(c, int) and c >= FULL - 1:
                        dve.wait_ge(w3_stored, 16 * c)
                    if kind == 0:
                        dve.wait_ge(w12_lo, 2 * c + 2)
                    if kind == 2 and not (isinstance(c, int) and c >= FULL - 1):
                        dve.wait_ge(w12_lo, 2 * c + 3)
                    if kind == 2:
                        loads = 2 * c + 2 if rows == P else 2 * c + 1
                        combine(n, npar, first, S3[0:rows, :], s3_loaded, 16 * loads, rows)
                    else:
                        combine(n, npar, first, S12[kind][:], s12_loaded[kind], 16 * (c + 2))
                    if i > 0 and seq[i - 1] != 2:
                        prev = seq[i - 1]
                        dve.wait_ge(stage_done, c + 1)
                        w12_low(n - 1, (npar + 1) % 2, 2 * ((cpar + 1) % 2) + prev, 2 * c + 3 + prev)
                    make_h(c, i)
                for b in range(len(seq), TPB):
                    make_h(c, b)

            up_step(0, 0)
            up_step(1, 1)
            with dve.Fori(1, PAIRS) as i:
                up_step(2 * i, 0)
                up_step(2 * i + 1, 1)
            for c in range(2 * PAIRS, FULL):
                up_step(c, c % 2)
            c = FULL
            n = number(c, 2)
            dve.wait_ge(w3_stored, 16 * c)
            dve.wait_ge(w12_lo, 2 * FULL + 1)
            combine(n, n % 2, NL * n, S3[0:TAIL, :], s3_loaded, 16 * (2 * c + 1), TAIL)

            def low(tb, ch, par, with_w3):
                rows = TAIL if isinstance(ch, int) and ch == CH - 1 else P
                g = tb * CH + ch
                dve.wait_ge(h_hi, g + 1)
                if not (isinstance(g, int) and g < 2):
                    dve.wait_ge(h_used, g - 1)
                dve.tensor_tensor(HLO[par][0:rows, :], HR[par][0:rows, :], HHI[par][0:rows, :].bitcast(F32),
                                  ALU.subtract).then_inc(h_lo, 1)
                if with_w3:
                    dve.wait_ge(w3_hi, ch + 1)
                    dve.tensor_tensor(w3_low_part(ch)[0:rows, :], W3R[par][0:rows, :], W3H[0:rows, ch, :].bitcast(F32),
                                      ALU.subtract).then_inc(w3_lo, 1)

            def out_tile(tb, k):
                t = TPB * tb + k
                if k < TPB - 1:
                    dve.wait_ge(block_done, (TPB - 1) * tb + k + 1)
                else:
                    dve.wait_ge(h_used, CH * (tb + 1))
                if k == 0:
                    dve.wait_ge(gb_loaded, 16 * (tb + 1))
                y = ps[:, 2 * k:2 * k + 2, :].rearrange("p a n -> p (a n)")
                if not (isinstance(t, int) and t == 0):
                    dve.wait_ge(out_made, t)
                dve.tensor_tensor(YG[:], y, GB[:], ALU.mult).then_inc(y_gated, 1)
                dve.wait_ge(y_gated, t + 1)
                dve.wait_ge(x2_loaded[k % 2], 16 * (2 * tb + k // 2 + 1))
                dve.tensor_tensor(X2[k % 2][:], X2[k % 2][:], YG[:], ALU.add).then_inc(out_made, 1)

            def down_low(tb, with_w3, more):
                with dve.Fori(1, CH // 2 - 2) as i:
                    for k in range(2):
                        low(tb, 2 * i + k, k, with_w3)
                for ch in range(CH - 4, CH):
                    low(tb, ch, ch % 2, with_w3)
                if more:
                    low(tb + 1, 0, 0, False)
                out_tile(tb, 0)
                out_tile(tb, 1)
                if more:
                    low(tb + 1, 1, 1, False)
                out_tile(tb, 2)
                out_tile(tb, 3)

            make_h(c, 0)
            make_h(c, 1)
            dve.wait_ge(w3_stored, 16 * CH)
            dve.wait_ge(up_done, (TPB - 1) * FULL + 2)
            low(0, 0, 0, True)
            make_h(c, 2)
            low(0, 1, 1, True)
            make_h(c, 3)
            dve.wait_ge(stage_done, 1 + CH)
            down_low(0, True, True)
            with dve.Fori(1, BATCH - 1) as tb:
                down_low(tb, False, True)
            down_low(BATCH - 1, False, False)

        @block.tensor
        def _(pe):
            pe.wait_ge(silu_c_made, 1)

            def modulation(j):
                m, half = j // 2, j % 2
                pe.wait_ge(wmod_loaded[j % 3], 16 * (j // 3 + 1))
                if half == 0:
                    if m == 3:
                        pe.wait_ge(gate_step, 2)
                    elif m == 4:
                        pe.wait_ge(gate_out, 1)
                    elif m == 5:
                        pe.wait_ge(mod_read, 3)
                pattern = "k (f p) -> k f p" if m % 3 == 2 else "k (p f) -> k f p"
                for f in range(C):
                    for cc in range(C // 2):
                        last = pe.matmul(ps[:, MOD_BANK[m], f * BATCH:(f + 1) * BATCH],
                                         WM[j % 3][:, cc, :].rearrange(pattern, f=C)[:, f, :],
                                         SC[:, 4 * half + cc, :],
                                         start=(half == 0 and f == 0 and cc == 0), stop=(half == 1 and cc == 3),
                                         skip_group_check=True)
                last.then_inc(wmod_used, 1)

            def turn_gate(g):
                pe.wait_ge(gate_step, GATE_STEPS * (g + 1))
                if g:
                    pe.wait_ge(mod_read, 4)
                pe.transpose(ps[0:BATCH * C, GATE_BANK, 0:P], MAG[:], IDENT[:]).then_inc(gate_turned, 1)

            def turn(bank, src, done):
                for c in range(C):
                    last = pe.transpose(ps[:, bank + c // 4, (c % 4) * P:(c % 4 + 1) * P],
                                        src.rearrange("t (p c) -> t c p", c=C)[:, c, :], IDENT[:])
                last.then_inc(done, 1)

            def turn1(t):
                pe.wait_ge(normed1, t + 1)
                if t >= 1:
                    pe.wait_ge(modulated1, t)
                turn(4, XN[t % 2][:], turned1)

            def turn2(e):
                if e < HALF_TILES:
                    t = e + HALF_TILES
                    if e == 0:
                        pe.wait_ge(gate_out, 2)
                    else:
                        pe.wait_ge(modulated2, e)
                    pe.wait_ge(ln2_step, LN_STEPS * (t + 1))
                    turn(6, XN2[t % 2][:], turned2)
                else:
                    d = e - HALF_TILES
                    pe.wait_ge(xn2_loaded[d % TPB], 16 * (d // TPB + 1))
                    if d == 0:
                        pe.wait_ge(modulated1, TILES)
                    else:
                        pe.wait_ge(modulated2, e if d == 1 else e - 1)
                    turn(4 + 2 * (e % 2), X[d % TPB][:], turned2)

            def attend(t):
                par = t % 2
                pe.wait_ge(low1, t + 1)
                if t >= 2:
                    pe.wait_ge(gated, t - 1)
                for hb in range(2):
                    acc = ps[:, 2 * par + hb, :]
                    cols = slice(hb * HALF, (hb + 1) * HALF)
                    for c in range(C):
                        pe.matmul(acc, AH[par][:, c, :], WH[:, c, cols], start=(c == 0), stop=False)
                        pe.matmul(acc, AH[par][:, c, :], WL[:, c, cols], start=False, stop=False)
                        last = pe.matmul(acc, AL[par][:, c, :], WH[:, c, cols], start=False, stop=(c == C - 1))
                last.then_inc(attn_done, 1)

            for j in range(4):
                modulation(j)
                if j == 1:
                    pe.wait_ge(consts_made, 2)
                    pe.wait_ge(mask_step, 5)
                    pe.matmul(ps[:, MASK_BANK, 0:D // MASK_B], GROUP[:], MCOL[:], start=True, stop=True).then_inc(mask_summed, 1)
            turn1(0)
            pe.wait_ge(w_lo, 4)
            for t in range(TILES):
                if t + 1 < TILES:
                    turn1(t + 1)
                if t == 1:
                    turn_gate(0)
                if t == 8:
                    turn_gate(1)
                attend(t)
                if t == 0:
                    modulation(4)
                    modulation(5)
                elif t <= 6:
                    modulation(5 + t)
                if t - 1 >= HALF_TILES:
                    turn2(t - 1 - HALF_TILES)
            pe.wait_ge(attn_done, TILES)
            pe.sem_inc(stage_done, 1)

            TURN_BEFORE = [[], [7, 8], [9, 10], [11, 12], [13, 14, 15], [], [], []]

            def up_block(c, cpar, b):
                banks = [2 * b, 2 * b + 1]
                if isinstance(c, int) and c == 0:
                    for e in TURN_BEFORE[2 * b]:
                        turn2(e)
                    pe.wait_ge(low2, TPB * (b + 1))
                    if b < 2:
                        pe.wait_ge(gated, TILES - 1 + b)
                    else:
                        pe.wait_ge(modulated2, TILES)
                else:
                    pe.wait_ge(h_made, TPB * c + b + 1)
                for w in range(2):
                    if isinstance(c, int) and c == 0 and w == 1:
                        for e in TURN_BEFORE[2 * b + 1]:
                            turn2(e)
                    ring = 2 * cpar + w
                    if b == 0:
                        pe.wait_ge(w12_lo, 2 * c + w + 1)
                    for k in range(C):
                        acc = ps[:, banks[w], :]
                        pe.matmul(acc, RH[ring][:, k, :], HH[:, b, k, :], start=(k == 0), stop=False)
                        pe.matmul(acc, RH[ring][:, k, :], HL[:, b, k, :], start=False, stop=False)
                        last = pe.matmul(acc, RL[ring][:, k, :], HH[:, b, k, :], start=False, stop=(k == C - 1))
                return last

            def up_step(c, cpar):
                for b in range(TPB):
                    up_block(c, cpar, b).then_inc(up_done if b < TPB - 1 else stage_done, 1)

            up_step(0, 0)
            up_step(1, 1)
            with pe.Fori(1, PAIRS) as i:
                up_step(2 * i, 0)
                up_step(2 * i + 1, 1)
            for c in range(2 * PAIRS, FULL):
                up_step(c, c % 2)
            c, ring = FULL, 2 * (FULL % 2)
            pe.wait_ge(w12_lo, 2 * FULL + 1)
            for b in range(TPB):
                pe.wait_ge(h_made, TPB * c + b + 1)
                acc = ps[:, 2 * b, :]
                for k in range(C):
                    pe.matmul(acc, RH[ring][:, k, :], HH[:, b, k, :], start=(k == 0), stop=False)
                    pe.matmul(acc, RH[ring][:, k, :], HL[:, b, k, :], start=False, stop=False)
                    last = pe.matmul(acc, RL[ring][:, k, :], HH[:, b, k, :], start=False, stop=(k == C - 1))
                last.then_inc(up_done if b < TPB - 1 else stage_done, 1)

            def down_chunk(tb, ch, par, with_w3):
                rows = TAIL if isinstance(ch, int) and ch == CH - 1 else P
                first, final = isinstance(ch, int) and ch == 0, isinstance(ch, int) and ch == CH - 1
                g = tb * CH + ch
                pe.wait_ge(h_lo, g + 1)
                if with_w3:
                    pe.wait_ge(w3_lo, ch + 1)
                for k in range(TPB):
                    if first:
                        if isinstance(tb, int):
                            pe.wait_ge(h_made, TPB * CH + k + 1)
                        else:
                            pe.wait_ge(y_gated, TPB * (tb - 1) + k + 1)
                    tok = slice(k * P, (k + 1) * P)
                    hi, lo = HHI[par][0:rows, tok], HLO[par][0:rows, tok]
                    w_hi_part, w_lo_part = W3H[:, ch, :], w3_low_part(ch)
                    for i, (lhs, w) in enumerate(((hi, w_hi_part), (hi, w_lo_part), (lo, w_hi_part))):
                        for hb in range(2):
                            last = pe.matmul(ps[:, 2 * k + hb, :], lhs, w[0:rows, hb * HALF:(hb + 1) * HALF],
                                             start=(first and i == 0), stop=(final and i == 2))
                    if final and k < TPB - 1:
                        last.then_inc(block_done, 1)
                last.then_inc(h_used, 1)

            def down(tb, with_w3):
                for ch in range(2):
                    down_chunk(tb, ch, ch, with_w3)
                with pe.Fori(1, CH // 2 - 2) as i:
                    for k in range(2):
                        down_chunk(tb, 2 * i + k, k, with_w3)
                for ch in range(CH - 4, CH):
                    down_chunk(tb, ch, ch % 2, with_w3)

            down(0, True)
            with pe.Fori(1, BATCH) as tb:
                down(tb, False)


def kernel(**inputs):
    import concourse.bacc as bacc
    from concourse.bass_utils import run_bass_kernel_spmd

    a = {k: np.asarray(v) for k, v in inputs.items()}
    w1, w2 = a["L0_ffn_w1_q"].T, a["L0_ffn_w2_q"].T
    s1, s2 = a["L0_ffn_w1_scale"].T, a["L0_ffn_w2_scale"].T

    def tiles(m, rows):
        full = m[:, :FULL * P].reshape(rows, -1, FULL, P)
        return full.transpose(2, 0, 1, 3)

    def pairs(m1, m2, rows):
        both = np.stack([tiles(m1, rows), tiles(m2, rows)], axis=1)
        both = both.reshape(2 * FULL, rows, -1, P)
        tail = np.concatenate([m1[:, FULL * P:].reshape(rows, -1, TAIL), m2[:, FULL * P:].reshape(rows, -1, TAIL)], axis=2)
        return np.ascontiguousarray(np.concatenate([both, tail[None]], axis=0).reshape(2 * FULL + 1, rows, -1))

    arrays = {
        "cT": np.ascontiguousarray(a["L0_c"].T).reshape(P, C * BATCH),
        "x": a["L0_attn_data"].reshape(TOK, D),
        "w12q": pairs(w1, w2, P),
        "w12s": pairs(s1, s2, D // NF4B),
        "w3q": np.ascontiguousarray(a["L0_ffn_w3_q"].T),
        "w3s": np.ascontiguousarray(a["L0_ffn_w3_scale"].T),
        "wT": np.ascontiguousarray(a["L0_attn_weight"].T),
        "maskT": np.ascontiguousarray(a["L0_attn_mask"].T),
        "wmod": a["L0_wmod"],
    }
    nc = bacc.Bacc("TRN2", target_bir_lowering=False, num_devices=1)
    args = [nc.dram_tensor(n, v.shape, mybir.dt.from_np(v.dtype), kind="ExternalInput").ap() for n, v in arrays.items()]
    out = nc.dram_tensor("out", (TOK, D), F32, kind="ExternalOutput").ap()
    adaln_kernel(nc, *args, out)
    r = run_bass_kernel_spmd(nc, [arrays], core_ids=[0])
    return r.results[0]["out"].reshape(BATCH, SEQ, D)
```

```python
import numpy as np
import concourse.bass as bass
from concourse import mybir

F32, F32R, I32 = mybir.dt.float32, mybir.dt.float32r, mybir.dt.int32
ALU, ACT, AXL = mybir.AluOpType, mybir.ActivationFunctionType, mybir.AxisListType

P = 128
BATCH, SEQ, D, HID = 4, 512, 1024, 2752
TOK = BATCH * SEQ
TILES = TOK // P
TPB = SEQ // P
C = D // P
NF4B = 64
FULL = HID // P
CH = FULL + 1
PAIRS = FULL // 2 - 1
LOWER = 18
TAIL = HID - FULL * P
HALF = 512
MASK_B = 32
EPS = 1e-5
KB = 1024

NF4 = [-1.0, -0.6961928009986877, -0.5250730514526367, -0.39491748809814453, -0.28444138169288635,
       -0.18477343022823334, -0.09105003625154495, 0.0, 0.07958029955625534, 0.16093020141124725,
       0.24611230194568634, 0.33791524171829224, 0.44070982933044434, 0.5626170039176941, 0.7229568362236023, 1.0]


def nf4_lines():
    table = np.array(NF4, np.float32).astype(np.float64)
    lines = []
    for q in range(0, 16, 2):
        best = None
        slope = np.float32(table[q + 1] - table[q])
        for da in range(-40, 41):
            a = np.float32(slope + da * np.spacing(slope))
            offset = np.float32(table[q] - np.float64(a) * q)
            for db in (-1, 0, 1):
                b = np.float32(offset + db * np.spacing(offset))
                got = [float(np.float32(np.float64(a) * k + np.float64(b))) for k in (q, q + 1)]
                off = [abs(got[0] - table[q]), abs(got[1] - table[q + 1])]
                if q == 6:
                    off[1] = 0.0 if got[1] >= 0 else 1.0
                key = (max(off), sum(off), abs(da))
                if best is None or key < best[0]:
                    best = (key, float(a), float(b))
        lines.append(best[1:])
    return lines


LINES = [nf4_lines()[i] for i in (0, 1, 4, 5, 2, 6, 3, 7)]
NL = len(LINES)
READ_BY = [0, 0, 1, 1, 2, 3, 4, 5]
LSLOTS = 3
CSTEPS = 8


def adaln_kernel(nc, cT, x, w12q, w12s, w3q, w3s, wT, maskT, wmod, out):
    base = (nc.sbuf_base + 31) // 32 * 32

    def at(name, shape, dt, kb):
        return nc.alloc_sbuf_tensor_at(name, [P] + shape, dt, offset=base + int(kb * KB))

    HH = at("ffn_in_hi", [BATCH, C, SEQ], F32R, 0)
    HL = at("ffn_in_lo", [BATCH, C, SEQ], F32R, 64)
    WH = at("attn_w_hi", [C, D], F32R, 32)
    WL = at("attn_w_lo", [C, D], F32R, 96)
    WM = [at(f"wmod_{i}", [C // 2, D], F32, kb) for i, kb in enumerate((0, 16, 64))]
    MP = [at(f"mask_piece_{i}", [2, D], I32, 96 + 8 * i) for i in range(4)]
    WP = [at(f"weight_piece_{i}", [2, D], F32, kb) for i, kb in enumerate((80, 88, 136, 152))]
    RH = [at(f"w12_hi_{i}", [C, P], F32R, 128 + 4 * i) for i in range(4)]
    RL = [at(f"w12_lo_{i}", [C, P], F32R, 144 + 4 * i) for i in range(4)]
    AH = [at(f"attn_in_hi_{i}", [C, P], F32R, 136 + 4 * i) for i in range(2)]
    AL = [at(f"attn_in_lo_{i}", [C, P], F32R, 152 + 4 * i) for i in range(2)]
    ST = 160
    Q = [at(f"codes_{i}", [C * P], I32, ST + 4 * i) for i in range(2)]
    ACC = [at(f"decoded_{i}", [C * P], F32, ST + 8 + 4 * i) for i in range(2)]
    POS = at("positive_part", [C * P], F32, ST + 16)
    L = [at(f"line_{i}", [C * P], F32, ST + 20 + 4 * i) for i in range(LSLOTS)]
    S12 = [at(f"w12_scale_{i}", [P], F32, ST + 32 + 0.5 * i) for i in range(2)]
    S3 = at("w3_scale", [D], F32, ST + 33)
    SG = at("silu_g", [HALF], F32, ST + 37)
    HT = [at(f"h_tile_{i}", [HALF], F32, ST + 39 + 2 * i) for i in range(2)]
    X = [at(f"x_{i}", [D], F32, ST + 4 * i) for i in range(4)]
    XN = [at(f"normed_{i}", [D], F32, ST + 16 + 4 * i) for i in range(2)]
    HM = [at(f"modulated_{i}", [C, P], F32, ST + 24 + 4 * i) for i in range(2)]
    GA = at("attn_gate", [D], F32, ST + 32)
    XN2 = [at(f"normed_again_{i}", [D], F32, ST + 36 + 4 * i) for i in range(2)]
    VEC = [at(f"mod_rows_{i}", [D], F32, kb) for i, kb in enumerate((ST + 36, 80))]
    SGN, MAG = at("gate_sign", [D], F32, 84), at("gate", [D], F32, 88)
    MSUM = at("mask_sums", [C, D // MASK_B], F32, ST + 40)
    MCOL, BMASK = (at(n, [D // MASK_B], F32, ST + kb) for n, kb in (("mask_column", 41), ("block_mask", 41.25)))
    W3H = at("w3_hi", [CH, D], F32R, 0)
    W3L = at("w3_lo", [LOWER, D], F32R, 88)
    W3LT = at("w3_lo_top", [FULL - LOWER, D], F32R, 195.75)
    DN = 160
    HR = [at(f"h_raw_{i}", [HALF], F32, DN + 2 * i) for i in range(2)]
    HHI = [at(f"h_hi_{i}", [HALF], F32R, DN + 4 + 2 * i) for i in range(2)]
    HLO = [at(f"h_lo_{i}", [HALF], F32R, DN + 8 + 2 * i) for i in range(2)]
    GB = at("ffn_gate", [D], F32, DN + 12)
    YG = [at(f"gated_{i}", [D], F32, DN + 16 + 4 * i) for i in range(2)]
    X2 = [at(f"x2_{i}", [D], F32, kb) for i, kb in enumerate((DN + 24, DN + 28, 0, 4))]
    W3R = [at(f"w3_raw_{i}", [D], F32, DN + 24 + 4 * i) for i in range(2)]

    def w3_low_part(ch):
        return W3LT[:, ch - LOWER, :] if isinstance(ch, int) and ch >= LOWER else W3L[:, ch, :]

    free = [ST + 44]

    def small(name, shape, dt=F32):
        t = at(name, shape, dt, free[0])
        free[0] += (int(np.prod(shape)) * 4 + 31) // 32 * 32 / KB
        return t

    IDENT = small("identity", [P])
    GROUP = small("four_partition_groups", [P])
    CT, SC = small("c", [C, BATCH]), small("silu_c", [C, BATCH])
    MODS = [small(f"mod_{i}", [BATCH, 2 * C]) for i in range(2)]
    STATS = [[small(f"stats_{k}{i}", [12]) for i in range(2)] for k in range(2)]
    MV = [[small(f"mean_var_{k}{i}", [2]) for i in range(2)] for k in range(2)]
    VE = [[small(f"var_eps_{k}{i}", [1]) for i in range(2)] for k in range(2)]
    SD = [[small(f"std_{k}{i}", [1]) for i in range(2)] for k in range(2)]
    RS = [[small(f"rstd_{k}{i}", [1]) for i in range(2)] for k in range(2)]
    T1 = [[small(f"newton_{k}{i}", [1]) for i in range(2)] for k in range(2)]
    T2 = [[small(f"newton_factor_{k}{i}", [1]) for i in range(2)] for k in range(2)]
    NB = [small(f"neg_mean_rstd_{i}", [1]) for i in range(2)]
    RF = [[small(f"rstd_fine_{k}{i}", [1]) for i in range(2)] for k in range(2)]

    ps = nc.alloc_psum_tensor("ps", [P, 8, HALF], F32)

    gates_d = nc.dram_tensor("gates_d", (2, BATCH, D), F32, kind="Internal").ap()
    x2_d = nc.dram_tensor("x2_d", (TOK, D), F32, kind="Internal").ap()
    xn2_d = nc.dram_tensor("xn2_d", (TOK, D), F32, kind="Internal").ap()
    h_d = nc.dram_tensor("h_d", (CH * P, TOK), F32, kind="Internal").ap()
    w3_d = nc.dram_tensor("w3_d", (CH * P, D), F32, kind="Internal").ap()

    sem = nc.alloc_semaphore
    c_loaded, ga_loaded, gb_loaded = sem("c_loaded"), sem("ga_loaded"), sem("gb_loaded")
    gate_stored = sem("gate_stored")
    codes_loaded = [sem(f"codes_loaded_{i}") for i in range(2)]
    s12_loaded = [sem(f"s12_loaded_{i}") for i in range(2)]
    s3_loaded = sem("s3_loaded")
    wmod_loaded = [sem(f"wmod_loaded_{i}") for i in range(3)]
    mask_loaded = [sem(f"mask_loaded_{i}") for i in range(4)]
    weight_loaded = [sem(f"weight_loaded_{i}") for i in range(4)]
    x_loaded = [sem(f"x_loaded_{i}") for i in range(4)]
    x2_stored = [sem(f"x2_stored_{i}") for i in range(4)]
    xn2_stored = [sem(f"xn2_stored_{i}") for i in range(2)]
    xn2_loaded = [sem(f"xn2_loaded_{i}") for i in range(4)]
    h_stored = [sem(f"h_stored_{i}") for i in range(2)]
    w3_stored = sem("w3_stored")
    h_loaded = [sem(f"h_loaded_{i}") for i in range(2)]
    w3_loaded = [sem(f"w3_loaded_{i}") for i in range(2)]
    x2_loaded = [sem(f"x2_loaded_{i}") for i in range(4)]
    out_stored = [sem(f"out_stored_{i}") for i in range(2)]
    consts_made = sem("consts_made")
    pool_step = sem("pool_step")
    silu_c_made = sem("silu_c_made")
    wmod_used = sem("wmod_used")
    mod_read = sem("mod_read")
    gate_step = sem("gate_step")
    mask_step = sem("mask_step")
    mask_summed = sem("mask_summed")
    piece_masked = [sem(f"piece_masked_by_{e}") for e in ("pool", "dve")]
    w_hi = sem("w_hi")
    w_lo = sem("w_lo")
    line_ready = sem("line_ready")
    combined = sem("combined")
    w12_hi = sem("w12_hi")
    w12_lo = sem("w12_lo")
    ln1_step, ln2_step = sem("ln1_step"), sem("ln2_step")
    root1_done, root2_done = sem("root1_done"), sem("root2_done")
    normed1 = sem("normed1")
    turned1, turned2 = sem("turned1"), sem("turned2")
    modulated1, modulated2 = sem("modulated1"), sem("modulated2")
    half_modulated = sem("half_modulated")
    high1, high2 = sem("high1"), sem("high2")
    low1, low2 = sem("low1"), sem("low2")
    rows_read = sem("rows_read")
    mod_turned = sem("mod_turned")
    attn_done = sem("attn_done")
    gated = sem("gated")
    x2_made = sem("x2_made")
    stage_done = sem("stage_done")
    up_done = sem("up_done")
    silu_done = sem("silu_done")
    h_made = sem("h_made")
    h_hi, w3_hi = sem("h_hi"), sem("w3_hi")
    h_lo, w3_lo = sem("h_lo"), sem("w3_lo")
    block_done = sem("block_done")
    h_used = sem("h_used")
    y_gated = sem("y_gated")
    out_made = sem("out_made")

    MOD_BANK, TURN_BANK, MASK_BANK = (0, 6, 6, 6, 6, 6), {0: 3, 1: 0, 3: 6, 4: 6}, 2
    LN_STEPS, GATE_STEPS = 9, 5
    HALF_TILES = TILES // 2
    SHARED_FROM = HALF_TILES
    ORDER2 = list(range(HALF_TILES, TILES - 1)) + [0, TILES - 1] + list(range(1, HALF_TILES))

    def slot2(e):
        return 1 if e < HALF_TILES - 1 else (e + 1) % 2

    def place2(e):
        t = ORDER2[e]
        return batch_of(t), t % TPB

    def batch_of(t):
        return (t // TPB + BATCH // 2) % BATCH

    def rows_of(t):
        r = batch_of(t) * SEQ + (t % TPB) * P
        return slice(r, r + P)

    def first_n(c):
        return 2 + 3 * c

    def tiles_of(c):
        if isinstance(c, int) and c == FULL:
            return [2]
        if isinstance(c, int) and c == FULL - 1:
            return [0, 2]
        return [0, 1, 2]

    def number(c, kind):
        if isinstance(c, int) and c == FULL:
            return first_n(FULL - 1) + 2
        if isinstance(c, int) and c == FULL - 1 and kind == 2:
            return first_n(c) + 1
        return first_n(c) + kind

    block = nc.Block()
    with block:

        @block.sync
        def _(sp):
            sp.dma_start(CT[:], cT.rearrange("p (c b) -> p c b", b=BATCH)).then_inc(c_loaded, 16)
            wmod_v = wmod.rearrange("(p c) f -> p c f", c=C)

            def load_wmod(j):
                if j >= 3:
                    sp.wait_ge(wmod_used, j - 2)
                m, half = j // 2, j % 2
                sp.dma_start(WM[j % 3][:], wmod_v[:, 4 * half:4 * half + 4, m * D:(m + 1) * D]).then_inc(wmod_loaded[j % 3], 16)

            def load_codes(n, src, slot):
                sp.dma_start(Q[slot][0:src.shape[0], :], src).then_inc(codes_loaded[slot], 16)

            def load_s12(tile, w):
                src = w12s[tile].unsqueeze(1).broadcast_to([P // 8, 8, P])
                sp.dma_start(S12[w][:], src).then_inc(s12_loaded[w], 16)

            mask_v = maskT.rearrange("(p c) n -> p c n", c=C)
            weight_v = wT.rearrange("(p c) n -> p c n", c=C)

            def load_mask(j):
                sp.dma_start(MP[j][:], mask_v[:, 2 * j:2 * j + 2, :]).then_inc(mask_loaded[j], 16)

            def load_weight(j):
                sp.dma_start(WP[j][:], weight_v[:, 2 * j:2 * j + 2, :]).then_inc(weight_loaded[j], 16)

            def load_x(t):
                sp.dma_start(X[t][:], x[rows_of(t), :]).then_inc(x_loaded[t], 16)

            load_codes(0, w12q[0], 0)
            load_s12(0, 0)
            load_wmod(0)
            for j in range(4):
                load_mask(j)
            load_codes(1, w12q[1], 1)
            load_s12(1, 1)
            load_wmod(1)
            load_wmod(2)
            load_wmod(3)
            sp.wait_ge(line_ready, 2 * NL)
            load_x(0)
            load_x(1)
            for j in range(4):
                load_weight(j)
            sp.wait_ge(w12_lo, 2)
            load_x(2)
            load_x(3)
            for j in range(4, 9):
                load_wmod(j)

            def store_gate(g):
                sp.wait_ge(gate_step, GATE_STEPS * (g + 1))
                sp.dma_start(gates_d[g], MAG[0:BATCH, :]).then_inc(gate_stored, 16)

            def load_ga(b):
                sp.dma_start(GA[:], gates_d[0, b].partition_broadcast(P)).then_inc(ga_loaded, 16)

            store_gate(0)
            sp.wait_ge(gate_stored, 16)
            load_ga(batch_of(0))

            def load_normed(d):
                k = d % TPB
                if d < TPB:
                    sp.wait_ge(x2_stored[k], 16 * TILES // TPB)
                    if d < 2:
                        sp.wait_ge(xn2_stored[d], 16 * HALF_TILES // 2)
                else:
                    sp.wait_ge(turned2, ORDER2.index(d - TPB) + 1)
                sp.dma_start(X[k][:], xn2_d[rows_of(d), :]).then_inc(xn2_loaded[k], 16)

            for t in range(TILES):
                k = t % TPB
                if t > TILES - TPB:
                    load_normed(k - 1)
                sp.wait_ge(x2_made, t + 1)
                sp.dma_start(x2_d[rows_of(t), :], X[k][:]).then_inc(x2_stored[k], 16)
                if k == TPB - 1 and t < TILES - 1:
                    load_ga(batch_of(t + 1))
                sp.wait_ge(ln2_step, LN_STEPS * (t + 1))
                if t < HALF_TILES:
                    sp.dma_start(xn2_d[rows_of(t), :], XN2[t % 2][:]).then_inc(xn2_stored[t % 2], 16)
                if t + TPB < TILES:
                    sp.wait_ge(x2_stored[k], 16 * (t // TPB + 1))
                    sp.dma_start(X[k][:], x[rows_of(t + TPB), :]).then_inc(x_loaded[k], 16)
                if t in (0, 1, 5):
                    load_wmod({0: 9, 1: 10, 5: 11}[t])
                if t == HALF_TILES:
                    store_gate(1)
                    sp.wait_ge(gate_stored, 32)

            for d in range(TPB - 1, HALF_TILES):
                load_normed(d)

            def fetch(n, c, kind, slot):
                if kind == 2:
                    rows = TAIL if isinstance(c, int) and c == CH - 1 else P
                    load_codes(n, w3q[bass.ds(c * P, rows), :], slot)
                    for g in range(rows // NF4B):
                        sp.dma_start(S3[g * NF4B:(g + 1) * NF4B, :],
                                     w3s[2 * c + g].partition_broadcast(NF4B)).then_inc(s3_loaded, 16)
                else:
                    load_codes(n, w12q[2 * c + 2 + kind], slot)
                    load_s12(2 * c + 2 + kind, kind)

            def fetch_after(c, kind, par):
                n = number(c, kind)
                if kind == 2 and isinstance(c, int) and c >= FULL - 1:
                    sp.wait_ge(combined, CSTEPS * (number(c - 1, 2) + 1))
                else:
                    sp.wait_ge(combined, CSTEPS * (n - 2))
                sp.wait_ge(line_ready, NL * (n - 1))
                fetch(n, c, kind, par)

            def store_h(c, b):
                sp.wait_ge(h_made, TPB * (c + 1) + b + 1)
                rows = TAIL if isinstance(c, int) and c == FULL else P
                sp.dma_start(h_d[bass.ds(c * P, rows), b * HALF:(b + 1) * HALF],
                             HT[b % 2][0:rows, :]).then_inc(h_stored[b % 2], 16)

            def store_w3(c, par):
                n = number(c, 2)
                sp.wait_ge(combined, CSTEPS * (n + 1))
                rows = TAIL if isinstance(c, int) and c == FULL else P
                sp.dma_start(w3_d[bass.ds(c * P, rows), :], ACC[par][0:rows, :]).then_inc(w3_stored, 16)

            def chunk_rows(src, ch):
                if isinstance(ch, int) and ch == FULL:
                    return src[FULL * P:HID, :].unsqueeze(0).broadcast_to([2, TAIL, src.shape[1]])
                return src[bass.ds(ch * P, P), :]

            def load_h(tb, ch, par):
                g = tb * CH + ch
                if not (isinstance(tb, int) and tb == 0 and isinstance(ch, int) and ch < 2):
                    sp.wait_ge(h_lo, g - 1)
                sp.dma_start(HR[par][:], chunk_rows(h_d[:, bass.ds(tb * HALF, HALF)], ch)).then_inc(h_loaded[par], 16)

            def load_w3(ch, par):
                if not (isinstance(ch, int) and ch < 2):
                    sp.wait_ge(w3_lo, ch - 1)
                sp.dma_start(W3R[par][:], chunk_rows(w3_d, ch)).then_inc(w3_loaded[par], 16)

            def up_io(c, cpar):
                seq = tiles_of(c)
                par = {kind: (cpar + i) % 2 for i, kind in enumerate(seq)}
                if seq == [2]:
                    par = {2: (first_n(FULL - 1) + 2) % 2}
                nxt = c + 1
                last = isinstance(c, int) and c == FULL
                nseq = [] if last else tiles_of(nxt)
                if seq[-1] == 2 and len(seq) == 3:
                    fetch_after(c, 2, par[2])
                if last:
                    store_w3(c, par[2])
                store_h(c, 0)
                if last:
                    sp.wait_ge(w3_stored, 16 * CH)
                    sp.wait_ge(line_ready, NL * (number(FULL, 2) + 1))
                    sp.wait_ge(h_stored[0], 16 * (FULL * TPB // 2 + 1))
                    sp.wait_ge(h_stored[1], 16 * (FULL * TPB // 2))
                    for ch in range(2):
                        load_h(0, ch, ch)
                        load_w3(ch, ch)
                npar = {kind: (cpar + 1 + i) % 2 for i, kind in enumerate(nseq)}
                if nseq == [2]:
                    npar = {2: (first_n(FULL - 1) + 2) % 2}
                if nseq:
                    fetch_after(nxt, nseq[0], npar[nseq[0]])
                store_h(c, 1)
                if len(nseq) > 1:
                    fetch_after(nxt, nseq[1], npar[nseq[1]])
                if not last:
                    store_w3(c, par[2])
                store_h(c, 2)
                store_h(c, 3)

            sp.wait_ge(turned2, TILES - 2)
            sp.wait_ge(gated, TILES)
            for kind in range(2):
                fetch(first_n(0) + kind, 0, kind, kind)
            up_io(0, 0)
            up_io(1, 1)
            with sp.Fori(1, PAIRS) as i:
                up_io(2 * i, 0)
                up_io(2 * i + 1, 1)
            for c in range(2 * PAIRS, FULL):
                up_io(c, c % 2)
            up_io(FULL, FULL % 2)

            sp.wait_ge(stage_done, 1 + CH)
            for s in range(2):
                sp.wait_ge(h_stored[s], 16 * CH * TPB // 2)
            sp.wait_ge(w3_stored, 16 * CH)

            def store_out(tb, k):
                t = tb * TPB + k
                sp.wait_ge(out_made, t + 1)
                src = X2[k if isinstance(tb, int) and tb == BATCH - 1 else k % 2]
                sp.dma_start(out[bass.ds(t * P, P), :], src[:]).then_inc(out_stored[k % 2], 16)

            def load_x2(tb, k):
                if k >= 2 or not (isinstance(tb, int) and tb == 0):
                    sp.wait_ge(out_stored[k % 2], 16 * (tb * (TPB // 2) + k // 2))
                sp.dma_start(X2[k % 2][:], x2_d[bass.ds((tb * TPB + k) * P, P), :]).then_inc(x2_loaded[k % 2], 16)

            def down_io(tb, more):
                first = isinstance(tb, int) and tb == 0
                with sp.Fori(1 if first else 2, CH // 2 - 1) as i:
                    for k in range(2):
                        load_h(tb, 2 * i + k, k)
                        if first:
                            load_w3(2 * i + k, k)
                if not first:
                    sp.wait_ge(y_gated, tb * TPB)
                sp.dma_start(GB[:], gates_d[1, tb].partition_broadcast(P)).then_inc(gb_loaded, 16)
                if not first:
                    for k in range(2):
                        load_x2(tb, k)
                for ch in range(CH - 2, CH):
                    load_h(tb, ch, ch % 2)
                    if first:
                        load_w3(ch, ch % 2)
                if first:
                    for k in range(2):
                        sp.wait_ge(w3_lo, CH - 1 + k)
                        load_x2(tb, k)
                if more:
                    load_h(tb + 1, 0, 0)
                    load_h(tb + 1, 1, 1)
                else:
                    for k in range(2, TPB):
                        sp.wait_ge(h_used, CH * tb + k)
                        sp.dma_start(X2[k][:], x2_d[(tb * TPB + k) * P:(tb * TPB + k + 1) * P, :]).then_inc(x2_loaded[k], 16)
                store_out(tb, 0)
                if more:
                    load_h(tb + 1, 2, 0)
                    load_x2(tb, 2)
                store_out(tb, 1)
                if more:
                    load_h(tb + 1, 3, 1)
                    load_x2(tb, 3)
                store_out(tb, 2)
                store_out(tb, 3)

            down_io(0, True)
            with sp.Fori(1, BATCH - 1) as tb:
                down_io(tb, True)
            down_io(BATCH - 1, False)
            for s in range(2):
                sp.wait_ge(out_stored[s], 16 * TILES // 2)

        @block.gpsimd
        def _(pool):
            pool.memset(IDENT[:], 0.0).then_inc(pool_step, 1)
            pool.memset(GROUP[:], 1.0).then_inc(pool_step, 1)
            pool.wait_ge(pool_step, 2)
            pool.affine_select(out=IDENT[:], in_=IDENT[:], compare_op=ALU.not_equal, fill=1.0, base=0,
                               pattern=[[-1, P]], channel_multiplier=1).then_inc(consts_made, 1)
            g3 = GROUP[:].rearrange("p (g o) -> p g o", o=4)
            pool.affine_select(out=g3, in_=g3, compare_op=ALU.is_ge, fill=0.0, base=0,
                               pattern=[[-4, P // 4], [0, 4]], channel_multiplier=1).then_inc(pool_step, 1)
            pool.wait_ge(pool_step, 3)
            pool.affine_select(out=g3, in_=g3, compare_op=ALU.is_ge, fill=0.0, base=3,
                               pattern=[[4, P // 4], [0, 4]], channel_multiplier=-1).then_inc(consts_made, 1)
            pool.wait_ge(mask_step, 6)
            for j in (0, 2):
                pool.wait_ge(weight_loaded[j], 16)
                w4 = WP[j][:].rearrange("p c (n o) -> p c n o", o=MASK_B)
                pool.tensor_tensor(w4, w4, BMASK[:].unsqueeze(1).unsqueeze(3).broadcast_to([P, 2, D // MASK_B, MASK_B]),
                                   ALU.mult).then_inc(piece_masked[0], 1)

        def rows_in_psum(m):
            return ps[0:BATCH, MOD_BANK[m]:MOD_BANK[m] + 2, :].rearrange("p a n -> p (a n)")

        def line_free(eng, n, j):
            if j >= LSLOTS:
                eng.wait_ge(combined, CSTEPS * n + READ_BY[j - LSLOTS] + 1)
            elif not (isinstance(n, int) and n == 0):
                eng.wait_ge(combined, CSTEPS * (n - 1) + READ_BY[j - LSLOTS + NL] + 1)

        @block.scalar
        def _(act):
            act.wait_ge(c_loaded, 16)
            act.activation(SC[:], CT[:], ACT.Silu).then_inc(silu_c_made, 1)

            def lines(n, npar, first_line, codes_wait, rows=P):
                act.wait_ge(codes_loaded[npar], codes_wait)
                for j, (slope, offset) in enumerate(LINES):
                    line_free(act, n, j)
                    act.activation(L[(first_line + j) % LSLOTS][0:rows, :], Q[npar][0:rows, :], ACT.Copy,
                                   bias=offset, scale=slope).then_inc(line_ready, 1)

            def w12_high(n, npar, ring):
                act.wait_ge(combined, CSTEPS * (n + 1))
                act.activation(RH[ring][:], ACC[npar][:].rearrange("p (c h) -> p c h", c=C), ACT.Copy).then_inc(w12_hi, 1)

            for n in range(2):
                lines(n, n, NL * n, 16)
            for n in range(2):
                w12_high(n, n, n)
            def root(kind, t):
                step, done = ((ln1_step, root1_done), (ln2_step, root2_done))[kind]
                act.wait_ge(step, LN_STEPS * t + 4)
                act.activation(SD[kind][t % 2][:], VE[kind][t % 2][:], ACT.Sqrt).then_inc(done, 1)

            def norm1(t):
                act.wait_ge(ln1_step, LN_STEPS * (t + 1))
                if t >= 2:
                    act.wait_ge(turned1, t - 1)
                act.activation(XN[t % 2][:], X[t % TPB][:], ACT.Identity, bias=NB[t % 2][:],
                               scale=RF[0][t % 2][:]).then_inc(normed1, 1)

            def modulate(src, dst, mods, b, done, count, upto=C):
                for c in range(upto):
                    ins = act.activation(dst[:, c, :], ps[:, src + c // 4, (c % 4) * P:(c % 4 + 1) * P],
                                         ACT.Identity, bias=mods[:, b, c:c + 1], scale=mods[:, b, C + c:C + c + 1])
                ins.then_inc(done, 1)
                act.wait_ge(done, count)

            def input1(t):
                act.wait_ge(turned1, t + 1)
                if t >= 1:
                    act.wait_ge(low1, t)
                modulate(4, HM[0], MODS[0], batch_of(t), modulated1, t + 1)
                if t >= 2:
                    act.wait_ge(attn_done, t - 1)
                act.activation(AH[t % 2][:], HM[0][:], ACT.Copy).then_inc(high1, 1)

            def input2(e):
                s, (b, k) = slot2(e), place2(e)
                act.wait_ge(turned2, e + 1)
                if e == HALF_TILES - 1:
                    act.wait_ge(low1, TILES)
                    act.wait_ge(attn_done, TILES)
                elif e >= 1:
                    act.wait_ge(low2, e if e < HALF_TILES else e - 1)
                shared = e >= SHARED_FROM
                modulate(4 + 2 * s, HM[s], MODS[1], b, modulated2, e + 1, C // 2 if shared else C)
                if shared:
                    act.wait_ge(half_modulated, e - SHARED_FROM + 1)
                act.activation(HH[:, b, :, k * P:(k + 1) * P], HM[s][:], ACT.Copy).then_inc(high2, 1)

            def start1(t):
                root(0, t)
                norm1(t)

            def copy_rows(m):
                act.wait_ge(wmod_used, 2 * (m + 1))
                if m:
                    act.wait_ge(mod_turned, m)
                act.activation(VEC[0][0:BATCH, :], rows_in_psum(m), ACT.Copy).then_inc(rows_read, 1)

            copy_rows(0)
            for t in range(2):
                start1(t)
            for j in range(4):
                act.wait_ge(piece_masked[j % 2], j // 2 + 1)
                act.activation(WH[:, 2 * j:2 * j + 2, :], WP[j][:], ACT.Copy).then_inc(w_hi, 1)
                if j == 1:
                    copy_rows(1)
            act.wait_ge(mod_read, 2)
            input1(0)
            for t in range(TILES):
                if t == 1:
                    input1(2)
                    root(1, 0)
                else:
                    both = t - 2 >= HALF_TILES
                    if both:
                        input2(t - 2 - HALF_TILES)
                    elif t + 1 < TILES:
                        input1(t + 1)
                    if t >= 1:
                        root(1, t - 1)
                    if both and t + 1 < TILES:
                        input1(t + 1)
                if t + 2 < TILES:
                    start1(t + 2)
                if t == 9:
                    act.wait_ge(mod_read, 4)
            input2(HALF_TILES - 2)
            root(1, TILES - 1)
            for e in range(HALF_TILES - 1, TILES):
                input2(e)
            act.wait_ge(low2, TILES)

            def silu(c, b, rows=P):
                if b < TPB - 1:
                    act.wait_ge(up_done, (TPB - 1) * c + b + 1)
                else:
                    act.wait_ge(stage_done, c + 2)
                if not (isinstance(c, int) and c == 0 and b == 0):
                    act.wait_ge(h_made, TPB * (c + 1) + b)
                act.activation(SG[0:rows, :], ps[0:rows, 2 * b, :], ACT.Silu).then_inc(silu_done, 1)

            def up_step(c, cpar):
                seq = tiles_of(c)
                for i, kind in enumerate(seq):
                    n = number(c, kind)
                    npar = (cpar + i) % 2 if len(seq) > 1 else n % 2
                    rows = TAIL if seq == [2] else P
                    first = NL * number(c if isinstance(c, int) else cpar, kind)
                    lines(n, npar, first, codes_wait_value(n, npar), rows)
                    if isinstance(c, int) and c == 0:
                        if kind == 1:
                            for w in range(2):
                                w12_high(n - 1 + w, w, 2 + w)
                            for b in range(2):
                                silu(c, b)
                        elif kind == 2:
                            silu(c, i)
                        continue
                    if i > 0 and seq[i - 1] != 2:
                        prev = seq[i - 1]
                        act.wait_ge(stage_done, c + 1)
                        w12_high(n - 1, (npar + 1) % 2, 2 * ((cpar + 1) % 2) + prev)
                    silu(c, i)
                for b in range(len(seq), TPB):
                    silu(c, b, TAIL if seq == [2] else P)

            def codes_wait_value(n, npar):
                return 16 * (n // 2 + 1) if isinstance(n, int) else 8 * (n - npar) + 16

            up_step(0, 0)
            up_step(1, 1)
            with act.Fori(1, PAIRS) as i:
                up_step(2 * i, 0)
                up_step(2 * i + 1, 1)
            for c in range(2 * PAIRS, FULL):
                up_step(c, c % 2)
            c = FULL
            n = number(c, 2)
            lines(n, n % 2, NL * n, codes_wait_value(n, n % 2), TAIL)

            def high(tb, ch, par, with_w3):
                g = tb * CH + ch
                count = 16 * (tb * (CH // 2) + ch // 2 + 1) if isinstance(ch, int) else 16 * (tb * (CH // 2)) + 8 * (ch - par) + 16
                act.wait_ge(h_loaded[par], count)
                if not (isinstance(g, int) and g < 2):
                    act.wait_ge(h_used, g - 1)
                act.activation(HHI[par][:], HR[par][:], ACT.Copy).then_inc(h_hi, 1)
                if with_w3:
                    act.wait_ge(w3_loaded[par], count)
                    act.activation(W3H[:, ch, :], W3R[par][:], ACT.Copy).then_inc(w3_hi, 1)

            def down_high(tb, with_w3):
                if not with_w3:
                    for ch in range(2):
                        high(tb, ch, ch, with_w3)
                with act.Fori(1, CH // 2 - 1) as i:
                    for k in range(2):
                        high(tb, 2 * i + k, k, with_w3)
                for ch in range(CH - 2, CH):
                    high(tb, ch, ch % 2, with_w3)

            silu(c, 0, TAIL)
            silu(c, 1, TAIL)
            act.wait_ge(line_ready, NL * (n + 1))
            act.wait_ge(up_done, (TPB - 1) * FULL + 1)
            high(0, 0, 0, True)
            silu(c, 2, TAIL)
            high(0, 1, 1, True)
            silu(c, 3, TAIL)
            act.wait_ge(stage_done, 1 + CH)
            down_high(0, True)
            with act.Fori(1, BATCH) as tb:
                down_high(tb, False)

        @block.vector
        def _(dve):
            def combine(n, npar, first_line, scale, scale_sem, scale_count, rows=P):
                acc, pos = ACC[npar][0:rows, :], POS[0:rows, :]

                def line(j):
                    return L[(first_line + j) % LSLOTS][0:rows, :]

                def step(k, j, after):
                    dve.wait_ge(line_ready, NL * n + j + 1)
                    if not (isinstance(n, int) and n == 0 and after == 0):
                        dve.wait_ge(combined, CSTEPS * n + after)

                step(0, 1, 0)
                dve.tensor_tensor(acc, line(0), line(1), ALU.min).then_inc(combined, 1)
                step(1, 3, 0)
                dve.scalar_tensor_tensor(out=pos, in0=line(2), scalar=0.0, in1=line(3), op0=ALU.max, op1=ALU.max).then_inc(combined, 1)
                step(2, 4, 1)
                dve.scalar_tensor_tensor(out=acc, in0=line(4), scalar=0.0, in1=acc, op0=ALU.min, op1=ALU.min).then_inc(combined, 1)
                step(3, 5, 2)
                dve.tensor_tensor(pos, line(5), pos, ALU.max).then_inc(combined, 1)
                step(4, 6, 3)
                dve.tensor_tensor(acc, line(6), acc, ALU.min).then_inc(combined, 1)
                step(5, 7, 4)
                dve.tensor_tensor(pos, line(7), pos, ALU.max).then_inc(combined, 1)
                step(6, 7, 6)
                dve.tensor_tensor(acc, acc, pos, ALU.add).then_inc(combined, 1)
                step(7, 7, 7)
                dve.wait_ge(scale_sem, scale_count)
                if scale.shape[1] == P:
                    acc3 = acc.rearrange("p (c h) -> p c h", c=C)
                    dve.tensor_tensor(acc3, acc3, scale.unsqueeze(1).broadcast_to([P, C, P]), ALU.mult).then_inc(combined, 1)
                else:
                    dve.tensor_tensor(acc, acc, scale, ALU.mult).then_inc(combined, 1)

            def w12_low(n, npar, ring, count):
                dve.wait_ge(w12_hi, count)
                dve.wait_ge(combined, CSTEPS * (n + 1))
                dve.tensor_tensor(RL[ring][:], ACC[npar][:].rearrange("p (c h) -> p c h", c=C),
                                  RH[ring][:].bitcast(F32), ALU.subtract).then_inc(w12_lo, 1)

            def read_mod(m):
                ln, s = m // 3, m % 3
                dve.wait_ge(mod_turned, 2 * ln + s + 1)
                src = ps[:, TURN_BANK[m], 0:C * BATCH].rearrange("p (c b) -> p b c", b=BATCH)
                dve.tensor_scalar(MODS[ln][:, :, s * C:(s + 1) * C], src, float(s), None, ALU.add).then_inc(mod_read, 1)

            def copy_rows(m):
                dve.wait_ge(wmod_used, 2 * (m + 1))
                dve.wait_ge(mod_turned, m - 1)
                dve.tensor_copy(VEC[1][0:BATCH, :], rows_in_psum(m)).then_inc(rows_read, 1)

            def gate(g):
                dve.wait_ge(wmod_used, 6 * (g + 1))
                if g:
                    dve.wait_ge(gate_stored, 16 * g)
                src, sgn, mag = rows_in_psum(3 * g + 2), SGN[0:BATCH, :], MAG[0:BATCH, :]
                dve.tensor_scalar(sgn, src, 0.0, 2.0, ALU.is_ge, ALU.mult).then_inc(gate_step, 1)
                dve.tensor_copy(mag, src).then_inc(gate_step, 1)
                dve.wait_ge(gate_step, GATE_STEPS * g + 2)
                dve.scalar_tensor_tensor(out=mag, in0=mag, scalar=-1.0, in1=mag, op0=ALU.mult, op1=ALU.max).then_inc(gate_step, 1)
                dve.wait_ge(gate_step, GATE_STEPS * g + 3)
                dve.tensor_scalar(mag, mag, 0.25, None, ALU.max).then_inc(gate_step, 1)
                dve.wait_ge(gate_step, GATE_STEPS * g + 4)
                dve.scalar_tensor_tensor(out=mag, in0=sgn, scalar=-1.0, in1=mag, op0=ALU.add, op1=ALU.mult).then_inc(gate_step, 1)

            def statistics(kind, t, src):
                k, i = t % 2, LN_STEPS * t
                step = (ln1_step, ln2_step)[kind]
                st, mv, ve = STATS[kind][k], MV[kind][k], VE[kind][k]
                dve.bn_stats(st[:, 0:6], src[:, 0:HALF]).then_inc(step, 1)
                dve.bn_stats(st[:, 6:12], src[:, HALF:D]).then_inc(step, 1)
                dve.wait_ge(step, i + 2)
                dve.memset(ve[:], EPS)
                dve.bn_aggr(mv[:], st[:]).then_inc(step, 1)
                dve.wait_ge(step, i + 3)
                dve.tensor_tensor(ve[:], mv[:, 1:2], ve[:], ALU.add).then_inc(step, 1)

            def inverse_root(kind, t):
                k, i = t % 2, LN_STEPS * t
                step, done = ((ln1_step, root1_done), (ln2_step, root2_done))[kind]
                ve, sd, rs, t1, t2, rf = VE[kind][k], SD[kind][k], RS[kind][k], T1[kind][k], T2[kind][k], RF[kind][k]
                dve.wait_ge(done, t + 1)
                dve.reciprocal(rs[:], sd[:]).then_inc(step, 1)
                dve.wait_ge(step, i + 5)
                dve.scalar_tensor_tensor(out=t1[:], in0=rs[:], scalar=ve[:], in1=rs[:], op0=ALU.mult, op1=ALU.mult).then_inc(step, 1)
                dve.wait_ge(step, i + 6)
                dve.tensor_scalar(t2[:], t1[:], -0.5, 1.5, ALU.mult, ALU.add).then_inc(step, 1)
                dve.wait_ge(step, i + 7)
                if kind == 0 and t >= 2:
                    dve.wait_ge(normed1, t - 1)
                dve.tensor_tensor(rf[:], rs[:], t2[:], ALU.mult).then_inc(step, 1)
                dve.wait_ge(step, i + 8)

            def ln1_sums(t):
                dve.wait_ge(x_loaded[t % TPB], 16 * (t // TPB + 1))
                statistics(0, t, X[t % TPB][:])

            def ln1_factors(t):
                inverse_root(0, t)
                dve.scalar_tensor_tensor(out=NB[t % 2][:], in0=MV[0][t % 2][:, 0:1], scalar=-1.0, in1=RF[0][t % 2][:],
                                         op0=ALU.mult, op1=ALU.mult).then_inc(ln1_step, 1)

            def low_part1(t):
                dve.wait_ge(high1, t + 1)
                dve.tensor_tensor(AL[t % 2][:], HM[0][:], AH[t % 2][:].bitcast(F32), ALU.subtract).then_inc(low1, 1)

            def modulate_half(e):
                s, (b, _) = slot2(e), place2(e)
                dve.wait_ge(turned2, e + 1)
                dve.wait_ge(low2, e - 1)
                for c in range(C // 2, C):
                    ins = dve.tensor_scalar(HM[s][:, c, :], ps[:, 5 + 2 * s, (c % 4) * P:(c % 4 + 1) * P],
                                            MODS[1][:, b, C + c:C + c + 1], MODS[1][:, b, c:c + 1], ALU.mult, ALU.add)
                ins.then_inc(half_modulated, 1)

            def low_part2(e):
                s, (b, k) = slot2(e), place2(e)
                dve.wait_ge(high2, e + 1)
                dve.tensor_tensor(HL[:, b, :, k * P:(k + 1) * P], HM[s][:],
                                  HH[:, b, :, k * P:(k + 1) * P].bitcast(F32), ALU.subtract).then_inc(low2, 1)

            def residual(t):
                k, two = t % TPB, XN2[t % 2][:]
                dve.wait_ge(attn_done, t + 1)
                if k == 0:
                    dve.wait_ge(ga_loaded, 16 * (t // TPB + 1))
                if 2 <= t < HALF_TILES + 2:
                    dve.wait_ge(xn2_stored[t % 2], 16 * (t // 2))
                elif t >= 2:
                    dve.wait_ge(turned2, t - 1 - HALF_TILES)
                attn = ps[:, 2 * (t % 2):2 * (t % 2) + 2, :].rearrange("p a n -> p (a n)")
                dve.tensor_tensor(two, attn, GA[:], ALU.mult).then_inc(gated, 1)
                dve.wait_ge(gated, t + 1)
                dve.wait_ge(normed1, t + 1)
                dve.tensor_tensor(X[k][:], X[k][:], two, ALU.add).then_inc(x2_made, 1)
                dve.wait_ge(x2_made, t + 1)
                statistics(1, t, X[k][:])
                inverse_root(1, t)
                dve.tensor_scalar(two, X[k][:], MV[1][t % 2][:, 0:1], RF[1][t % 2][:], ALU.subtract, ALU.mult).then_inc(ln2_step, 1)

            def sum_mask(j):
                dve.wait_ge(mask_loaded[j], 16)
                dve.tensor_reduce(MSUM[:, 2 * j:2 * j + 2, :], MP[j][:].rearrange("p c (n o) -> p c n o", o=MASK_B),
                                  AXL.X, ALU.add).then_inc(mask_step, 1)

            def mask_weight(j):
                dve.wait_ge(weight_loaded[j], 16)
                w4 = WP[j][:].rearrange("p c (n o) -> p c n o", o=MASK_B)
                dve.tensor_tensor(w4, w4, BMASK[:].unsqueeze(1).unsqueeze(3).broadcast_to([P, 2, D // MASK_B, MASK_B]),
                                  ALU.mult).then_inc(piece_masked[1], 1)

            def split_weight(j):
                dve.wait_ge(w_hi, j + 1)
                dve.tensor_tensor(WL[:, 2 * j:2 * j + 2, :], WP[j][:], WH[:, 2 * j:2 * j + 2, :].bitcast(F32),
                                  ALU.subtract).then_inc(w_lo, 1)

            combine(0, 0, 0, S12[0][:], s12_loaded[0], 16)
            for j in range(4):
                sum_mask(j)
            dve.wait_ge(mask_step, 4)
            dve.tensor_reduce(MCOL[:], MSUM[:].rearrange("p c n -> p n c"), AXL.X, ALU.add).then_inc(mask_step, 1)
            dve.wait_ge(mask_summed, 1)
            dve.tensor_scalar(BMASK[:], ps[:, MASK_BANK, 0:D // MASK_B], 0.0, None, ALU.is_gt).then_inc(mask_step, 1)
            combine(1, 1, NL, S12[1][:], s12_loaded[1], 16)
            for n in range(2):
                w12_low(n, n, n, n + 1)
            dve.wait_ge(mask_step, 6)
            for t in range(2):
                ln1_sums(t)
                ln1_factors(t)
            mask_weight(1)
            split_weight(0)
            split_weight(1)
            mask_weight(3)
            split_weight(2)
            for m in range(2):
                read_mod(m)
            split_weight(3)

            dve.wait_ge(w_lo, 4)
            low_part1(0)
            for t in range(TILES):
                if t == 1:
                    gate(0)
                    low_part1(2)
                    residual(0)
                    ln1_sums(3)
                    ln1_factors(3)
                else:
                    if t >= 1:
                        residual(t - 1)
                    if t + 2 < TILES:
                        ln1_sums(t + 2)
                    if t - 2 >= HALF_TILES:
                        low_part2(t - 2 - HALF_TILES)
                    if t + 1 < TILES:
                        low_part1(t + 1)
                    if t + 2 < TILES:
                        ln1_factors(t + 2)
                if t in (3, 6):
                    copy_rows(t // 3 + 2)
                elif t in (4, 7):
                    read_mod(t // 3 + 2)
                elif t == 9:
                    gate(1)
            residual(TILES - 1)
            low_part2(SHARED_FROM - 2)
            for e in range(SHARED_FROM - 1, TILES):
                if e + 1 < TILES:
                    modulate_half(e + 1)
                low_part2(e)
            dve.wait_ge(turned2, TILES)
            dve.sem_inc(h_made, TPB)

            def make_h(c, b):
                dve.wait_ge(silu_done, TPB * c + b + 1)
                if not (isinstance(c, int) and c == 0 and b < 2):
                    dve.wait_ge(h_stored[b % 2], 16 * ((TPB // 2) * c + b // 2))
                if isinstance(c, int) and c == FULL:
                    dve.tensor_tensor(HT[b % 2][0:TAIL, :], SG[0:TAIL, :], ps[TAIL:2 * TAIL, 2 * b, :], ALU.mult).then_inc(h_made, 1)
                else:
                    dve.tensor_tensor(HT[b % 2][:], SG[:], ps[:, 2 * b + 1, :], ALU.mult).then_inc(h_made, 1)

            def up_step(c, cpar):
                seq = tiles_of(c)
                for i, kind in enumerate(seq):
                    n = number(c, kind)
                    npar = (cpar + i) % 2 if len(seq) > 1 else n % 2
                    rows = TAIL if seq == [2] else P
                    first = NL * number(c if isinstance(c, int) else cpar, kind)
                    if kind == 1 and not (isinstance(c, int) and c == 0):
                        dve.wait_ge(w3_stored, 16 * c)
                    if kind == 2 and isinstance(c, int) and c >= FULL - 1:
                        dve.wait_ge(w3_stored, 16 * c)
                    if kind == 0:
                        dve.wait_ge(w12_lo, 2 * c + 2)
                    if kind == 2 and not (isinstance(c, int) and c >= FULL - 1):
                        dve.wait_ge(w12_lo, 2 * c + 3)
                    if kind == 2:
                        loads = 2 * c + 2 if rows == P else 2 * c + 1
                        combine(n, npar, first, S3[0:rows, :], s3_loaded, 16 * loads, rows)
                    else:
                        combine(n, npar, first, S12[kind][:], s12_loaded[kind], 16 * (c + 2))
                    if isinstance(c, int) and c == 0:
                        if kind == 1:
                            for w in range(2):
                                w12_low(n - 1 + w, w, 2 + w, w + 3)
                            for b in range(2):
                                make_h(c, b)
                        elif kind == 2:
                            make_h(c, i)
                        continue
                    if i > 0 and seq[i - 1] != 2:
                        prev = seq[i - 1]
                        dve.wait_ge(stage_done, c + 1)
                        w12_low(n - 1, (npar + 1) % 2, 2 * ((cpar + 1) % 2) + prev, 2 * c + 3 + prev)
                    make_h(c, i)
                for b in range(len(seq), TPB):
                    make_h(c, b)

            up_step(0, 0)
            up_step(1, 1)
            with dve.Fori(1, PAIRS) as i:
                up_step(2 * i, 0)
                up_step(2 * i + 1, 1)
            for c in range(2 * PAIRS, FULL):
                up_step(c, c % 2)
            c = FULL
            n = number(c, 2)
            dve.wait_ge(w3_stored, 16 * c)
            dve.wait_ge(w12_lo, 2 * FULL + 1)
            combine(n, n % 2, NL * n, S3[0:TAIL, :], s3_loaded, 16 * (2 * c + 1), TAIL)

            def low(tb, ch, par, with_w3):
                rows = TAIL if isinstance(ch, int) and ch == CH - 1 else P
                g = tb * CH + ch
                dve.wait_ge(h_hi, g + 1)
                if not (isinstance(g, int) and g < 2):
                    dve.wait_ge(h_used, g - 1)
                dve.tensor_tensor(HLO[par][0:rows, :], HR[par][0:rows, :], HHI[par][0:rows, :].bitcast(F32),
                                  ALU.subtract).then_inc(h_lo, 1)
                if with_w3:
                    dve.wait_ge(w3_hi, ch + 1)
                    if rows == P:
                        dve.tensor_tensor(w3_low_part(ch), W3R[par][:], W3H[:, ch, :].bitcast(F32),
                                          ALU.subtract).then_inc(w3_lo, 1)
                    else:
                        dve.tensor_tensor(W3H[TAIL:P, ch, :], W3R[par][TAIL:P, :], W3H[TAIL:P, ch, :].bitcast(F32),
                                          ALU.subtract).then_inc(w3_lo, 1)

            def gate_tile(tb, k):
                t = TPB * tb + k
                if k < TPB - 1:
                    dve.wait_ge(block_done, (TPB - 1) * tb + k + 1)
                else:
                    dve.wait_ge(h_used, CH * (tb + 1))
                if k == 0:
                    dve.wait_ge(gb_loaded, 16 * (tb + 1))
                y = ps[:, 2 * k:2 * k + 2, :].rearrange("p a n -> p (a n)")
                if not (isinstance(t, int) and t < 2):
                    dve.wait_ge(out_made, t - 1)
                dve.tensor_tensor(YG[k % 2][:], y, GB[:], ALU.mult).then_inc(y_gated, 1)

            def out_tile(tb, k):
                t = TPB * tb + k
                dve.wait_ge(y_gated, t + 1)
                if isinstance(tb, int) and tb == BATCH - 1 and k >= 2:
                    s = k
                    dve.wait_ge(x2_loaded[s], 16)
                else:
                    s = k % 2
                    dve.wait_ge(x2_loaded[s], 16 * (2 * tb + k // 2 + 1))
                dve.tensor_tensor(X2[s][:], X2[s][:], YG[k % 2][:], ALU.add).then_inc(out_made, 1)

            def down_low(tb, with_w3, more):
                low(tb, 3, 1, with_w3)
                with dve.Fori(2, CH // 2 - 2) as i:
                    for k in range(2):
                        low(tb, 2 * i + k, k, with_w3)
                for ch in range(CH - 4, CH):
                    low(tb, ch, ch % 2, with_w3)
                if more:
                    low(tb + 1, 0, 0, False)
                gate_tile(tb, 0)
                gate_tile(tb, 1)
                for k in range(TPB - 2):
                    out_tile(tb, k)
                    gate_tile(tb, k + 2)
                if more:
                    low(tb + 1, 1, 1, False)
                    low(tb + 1, 2, 0, False)
                for k in range(TPB - 2, TPB):
                    out_tile(tb, k)

            make_h(c, 0)
            make_h(c, 1)
            dve.wait_ge(w3_stored, 16 * CH)
            dve.wait_ge(up_done, (TPB - 1) * FULL + 2)
            low(0, 0, 0, True)
            make_h(c, 2)
            low(0, 1, 1, True)
            make_h(c, 3)
            dve.wait_ge(stage_done, 1 + CH)
            low(0, 2, 0, True)
            down_low(0, True, True)
            with dve.Fori(1, BATCH - 1) as tb:
                down_low(tb, False, True)
            down_low(BATCH - 1, False, False)

        @block.tensor
        def _(pe):
            pe.wait_ge(silu_c_made, 1)

            def modulation(j):
                m, half = j // 2, j % 2
                pe.wait_ge(wmod_loaded[j % 3], 16 * (j // 3 + 1))
                if half == 0:
                    if m == 2:
                        pe.wait_ge(rows_read, 2)
                    elif m == 3:
                        pe.wait_ge(gate_step, 2)
                    elif m >= 4:
                        pe.wait_ge(mod_read, m - 1)
                for hb in range(2):
                    for cc in range(C // 2):
                        last = pe.matmul(ps[0:BATCH, MOD_BANK[m] + hb, :], SC[:, 4 * half + cc, :],
                                         WM[j % 3][:, cc, hb * HALF:(hb + 1) * HALF],
                                         start=(half == 0 and cc == 0), stop=(half == 1 and cc == 3))
                last.then_inc(wmod_used, 1)

            def turn_mod(m, i):
                pe.wait_ge(rows_read, i + 1)
                for c in range(C):
                    last = pe.transpose(ps[:, TURN_BANK[m], c * BATCH:(c + 1) * BATCH],
                                        VEC[m // 3][0:BATCH, :].rearrange("b (p c) -> b c p", c=C)[:, c, :],
                                        IDENT[0:BATCH, 0:BATCH])
                last.then_inc(mod_turned, 1)

            def turn(bank, src, done):
                for c in range(C):
                    last = pe.transpose(ps[:, bank + c // 4, (c % 4) * P:(c % 4 + 1) * P],
                                        src.rearrange("t (p c) -> t c p", c=C)[:, c, :], IDENT[:])
                last.then_inc(done, 1)

            def turn1(t):
                pe.wait_ge(normed1, t + 1)
                if t >= 1:
                    pe.wait_ge(modulated1, t)
                turn(4, XN[t % 2][:], turned1)

            def turn2(e):
                t = ORDER2[e]
                if e == 0:
                    pe.wait_ge(gate_step, GATE_STEPS + 2)
                elif e == HALF_TILES - 1:
                    pe.wait_ge(modulated1, TILES)
                else:
                    pe.wait_ge(modulated2, e if e < HALF_TILES - 1 else e - 1)
                if e - 2 >= SHARED_FROM:
                    pe.wait_ge(half_modulated, e - 1 - SHARED_FROM)
                if t >= HALF_TILES:
                    pe.wait_ge(ln2_step, LN_STEPS * (t + 1))
                    src = XN2[t % 2]
                else:
                    pe.wait_ge(xn2_loaded[t % TPB], 16 * (t // TPB + 1))
                    src = X[t % TPB]
                turn(4 + 2 * slot2(e), src[:], turned2)

            def attend(t):
                par = t % 2
                pe.wait_ge(low1, t + 1)
                if t >= 2:
                    pe.wait_ge(gated, t - 1)
                for hb in range(2):
                    acc = ps[:, 2 * par + hb, :]
                    cols = slice(hb * HALF, (hb + 1) * HALF)
                    for c in range(C):
                        pe.matmul(acc, AH[par][:, c, :], WH[:, c, cols], start=(c == 0), stop=False)
                        pe.matmul(acc, AH[par][:, c, :], WL[:, c, cols], start=False, stop=False)
                        last = pe.matmul(acc, AL[par][:, c, :], WH[:, c, cols], start=False, stop=(c == C - 1))
                last.then_inc(attn_done, 1)

            for j in range(4):
                modulation(j)
                if j == 0:
                    pe.wait_ge(consts_made, 2)
                    pe.wait_ge(mask_step, 5)
                    pe.matmul(ps[:, MASK_BANK, 0:D // MASK_B], GROUP[:], MCOL[:], start=True, stop=True).then_inc(mask_summed, 1)
                elif j == 2:
                    turn_mod(0, 0)
            turn_mod(1, 1)
            turn1(0)
            pe.wait_ge(w_lo, 4)
            for t in range(TILES):
                if t + 1 < TILES:
                    turn1(t + 1)
                if t in (4, 7):
                    turn_mod(t // 3 + 2, t // 3 + 1)
                attend(t)
                for j in {0: (4, 5), 1: (6,), 2: (7,), 5: (8, 9), 8: (10, 11)}.get(t, ()):
                    modulation(j)
                if t - 1 >= HALF_TILES:
                    turn2(t - 1 - HALF_TILES)
            turn2(HALF_TILES - 1)
            pe.wait_ge(attn_done, TILES)
            pe.sem_inc(stage_done, 1)

            TURN_AT = {(w, w ^ 1, k): HALF_TILES + 4 * w + k // 2 for w in range(2) for k in (0, 2, 4, 6)}

            def up_block(c, cpar, b):
                banks = [2 * b, 2 * b + 1]
                if isinstance(c, int) and c == 0:
                    pe.wait_ge(low2, HALF_TILES + 1 if b == 1 else TPB * (b + 1))
                    if b < 2:
                        pe.wait_ge(gated, TILES - 1 + b)
                    else:
                        pe.wait_ge(modulated2, TILES)
                        pe.wait_ge(half_modulated, TILES - SHARED_FROM)
                else:
                    pe.wait_ge(h_made, TPB * c + b + 1)
                for w in range(2):
                    ring = 2 * cpar + w
                    if b == 0:
                        pe.wait_ge(w12_lo, 2 * c + w + 1)
                    for k in range(C):
                        acc = ps[:, banks[w], :]
                        if isinstance(c, int) and c == 0 and (b, w, k) in TURN_AT:
                            turn2(TURN_AT[b, w, k])
                        pe.matmul(acc, RH[ring][:, k, :], HH[:, b, k, :], start=(k == 0), stop=False)
                        pe.matmul(acc, RH[ring][:, k, :], HL[:, b, k, :], start=False, stop=False)
                        last = pe.matmul(acc, RL[ring][:, k, :], HH[:, b, k, :], start=False, stop=(k == C - 1))
                return last

            def up_step(c, cpar):
                for b in range(TPB):
                    up_block(c, cpar, b).then_inc(up_done if b < TPB - 1 else stage_done, 1)

            up_step(0, 0)
            up_step(1, 1)
            with pe.Fori(1, PAIRS) as i:
                up_step(2 * i, 0)
                up_step(2 * i + 1, 1)
            for c in range(2 * PAIRS, FULL):
                up_step(c, c % 2)
            c, ring = FULL, 2 * (FULL % 2)
            pe.wait_ge(w12_lo, 2 * FULL + 1)
            for b in range(TPB):
                pe.wait_ge(h_made, TPB * c + b + 1)
                acc = ps[:, 2 * b, :]
                for k in range(C):
                    pe.matmul(acc, RH[ring][:, k, :], HH[:, b, k, :], start=(k == 0), stop=False)
                    pe.matmul(acc, RH[ring][:, k, :], HL[:, b, k, :], start=False, stop=False)
                    last = pe.matmul(acc, RL[ring][:, k, :], HH[:, b, k, :], start=False, stop=(k == C - 1))
                last.then_inc(up_done if b < TPB - 1 else stage_done, 1)

            def down_chunk(tb, ch, par, with_w3):
                rows = TAIL if isinstance(ch, int) and ch == CH - 1 else P
                first, final = isinstance(ch, int) and ch == 0, isinstance(ch, int) and ch == CH - 1
                g = tb * CH + ch
                pe.wait_ge(h_lo, g + 1)
                if with_w3:
                    pe.wait_ge(w3_lo, ch + 1)
                for k in range(TPB):
                    if first:
                        if isinstance(tb, int):
                            pe.wait_ge(h_made, TPB * CH + k + 1)
                        else:
                            pe.wait_ge(y_gated, TPB * (tb - 1) + k + 1)
                    tok = slice(k * P, (k + 1) * P)
                    hi, lo = HHI[par][:, tok], HLO[par][0:rows, tok]
                    if final:
                        passes = ((hi, W3H[:, ch, :]), (lo, W3H[0:rows, ch, :]))
                    else:
                        passes = ((hi, W3H[:, ch, :]), (hi, w3_low_part(ch)), (lo, W3H[:, ch, :]))
                    for i, (lhs, w) in enumerate(passes):
                        for hb in range(2):
                            last = pe.matmul(ps[:, 2 * k + hb, :], lhs, w[:, hb * HALF:(hb + 1) * HALF],
                                             start=(first and i == 0), stop=(final and i == 1))
                    if final and k < TPB - 1:
                        last.then_inc(block_done, 1)
                last.then_inc(h_used, 1)

            def down(tb, with_w3):
                for ch in range(2):
                    down_chunk(tb, ch, ch, with_w3)
                with pe.Fori(1, CH // 2 - 2) as i:
                    for k in range(2):
                        down_chunk(tb, 2 * i + k, k, with_w3)
                for ch in range(CH - 4, CH):
                    down_chunk(tb, ch, ch % 2, with_w3)

            down(0, True)
            with pe.Fori(1, BATCH) as tb:
                down(tb, False)


def kernel(**inputs):
    import concourse.bacc as bacc
    from concourse.bass_utils import run_bass_kernel_spmd

    a = {k: np.asarray(v) for k, v in inputs.items()}
    w1, w2 = a["L0_ffn_w1_q"].T, a["L0_ffn_w2_q"].T
    s1, s2 = a["L0_ffn_w1_scale"].T, a["L0_ffn_w2_scale"].T

    def tiles(m, rows):
        full = m[:, :FULL * P].reshape(rows, -1, FULL, P)
        return full.transpose(2, 0, 1, 3)

    def pairs(m1, m2, rows):
        both = np.stack([tiles(m1, rows), tiles(m2, rows)], axis=1)
        both = both.reshape(2 * FULL, rows, -1, P)
        tail = np.concatenate([m1[:, FULL * P:].reshape(rows, -1, TAIL), m2[:, FULL * P:].reshape(rows, -1, TAIL)], axis=2)
        return np.ascontiguousarray(np.concatenate([both, tail[None]], axis=0).reshape(2 * FULL + 1, rows, -1))

    arrays = {
        "cT": np.ascontiguousarray(a["L0_c"].T).reshape(P, C * BATCH),
        "x": a["L0_attn_data"].reshape(TOK, D),
        "w12q": pairs(w1, w2, P),
        "w12s": pairs(s1, s2, D // NF4B),
        "w3q": np.ascontiguousarray(a["L0_ffn_w3_q"].T),
        "w3s": np.ascontiguousarray(a["L0_ffn_w3_scale"].T),
        "wT": np.ascontiguousarray(a["L0_attn_weight"].T),
        "maskT": np.ascontiguousarray(a["L0_attn_mask"].T),
        "wmod": a["L0_wmod"],
    }
    nc = bacc.Bacc("TRN2", target_bir_lowering=False, num_devices=1)
    args = [nc.dram_tensor(n, v.shape, mybir.dt.from_np(v.dtype), kind="ExternalInput").ap() for n, v in arrays.items()]
    out = nc.dram_tensor("out", (TOK, D), F32, kind="ExternalOutput").ap()
    adaln_kernel(nc, *args, out)
    r = run_bass_kernel_spmd(nc, [arrays], core_ids=[0])
    return r.results[0]["out"].reshape(BATCH, SEQ, D)
```
